# Optimizing a Trainium2 kernel written in Bass

```python
import numpy as np
import jax
import jax.numpy as jnp

def _softmax(x, axis=-1):
    return jax.nn.softmax(x, axis=axis)

def _gelu(x):
    return jax.nn.gelu(x, approximate=True)

def _silu(x):
    return jax.nn.silu(x)

def _sigmoid(x):
    return jax.nn.sigmoid(x)

def _layernorm(x, axis=-1, eps=1e-05):
    m = jnp.mean(x, axis=axis, keepdims=True)
    v = jnp.var(x, axis=axis, keepdims=True)
    return (x - m) / jnp.sqrt(v + eps)

def _scatter_add(tgt, idx, src, axis=0):
    return tgt.at[idx].add(src)

def _segment_sum(src, seg, n):
    return jax.ops.segment_sum(src, seg, n)
kernel_name = 'mk_adj_resnorm_d4_adj_r2_218b69'

def setup_inputs(seed: int=0):
    np.random.seed(seed)
    _w = jnp.asarray

    def _rec_inputs():
        import jax
        import jax.numpy as jnp
        _gk = jax.random.key(seed)
        x = -0.0002928 + 1 * jax.random.normal(jax.random.fold_in(_gk, 1), (64, 128, 128), jnp.float32)
        _a = jax.random.bernoulli(jax.random.fold_in(_gk, 2), 0.125, (64, 128, 128))
        _a = jnp.logical_or(_a, jnp.swapaxes(_a, -1, -2))
        _a = jnp.logical_or(_a, jnp.eye(128, dtype=bool))
        adj = _a.astype(jnp.int32)
        _nm = jnp.ones((64, 128), dtype=bool)
        nodemask = jnp.where(_nm, 1.0, 0.0).astype(jnp.float32)
        return (x, adj, nodemask)
    x, adj, nodemask = _rec_inputs()

    def _L0_gnn_setup():
        import jax, jax.numpy as jnp
        import numpy as np
        IN_F = 128
        OUT_F = 128
        ALPHA = 0.2

        def _xavier(key, shape, gain=1.414):
            fan_in, fan_out = (shape[0], shape[1])
            limit = gain * np.sqrt(6.0 / (fan_in + fan_out))
            return jax.random.uniform(key, shape, jnp.float32, -limit, limit)
        key = jax.random.key(seed)
        k1, k2, k3, k4 = jax.random.split(key, 4)
        B, N = (8, 1024)
        h = jax.random.normal(k1, (B, N, IN_F), jnp.float32)
        adj = jax.random.randint(k2, (B, N, N), 0, 2, jnp.int32)
        W = _xavier(k3, (IN_F, OUT_F))
        a = _xavier(k4, (2 * OUT_F, 1))
        return {'h': h, 'adj': adj, 'W': W, 'a': a}
    _L0_gnn_all = _L0_gnn_setup()
    _L0_gnn_in = {k: v for k, v in _L0_gnn_all.items() if k in ('W', 'a')}
    del _L0_gnn_all

    def _L1_gnn_setup():
        import jax, jax.numpy as jnp
        import numpy as np
        EPS = 1e-05

        def _layernorm(x, w, b):
            m = jnp.mean(x, axis=-1, keepdims=True)
            v = jnp.mean((x - m) ** 2, axis=-1, keepdims=True)
            return (x - m) * jax.lax.rsqrt(v + EPS) * w + b

        def _swish(x):
            return x * jax.nn.sigmoid(x)
        key = jax.random.key(seed)
        ks = jax.random.split(key, 10)
        B, A, D_IN, D_OUT = (8, 1024, 128, 128)
        s_in = 1.0 / np.sqrt(D_IN)
        s_out = 1.0 / np.sqrt(D_OUT)
        return {'x': jax.random.normal(ks[0], (B, A, D_IN), dtype=jnp.float32), 'connectivity': jax.random.randint(ks[1], (B, A, A), 0, 2, dtype=jnp.int32), 'Wq': jax.random.uniform(ks[2], (D_OUT, D_IN), jnp.float32, -s_in, s_in), 'Wk': jax.random.uniform(ks[3], (D_OUT, D_IN), jnp.float32, -s_in, s_in), 'Wv': jax.random.uniform(ks[4], (D_OUT, D_IN), jnp.float32, -s_in, s_in), 'ln1_w': jnp.ones((D_OUT,), jnp.float32), 'ln1_b': jnp.zeros((D_OUT,), jnp.float32), 'W1': jax.random.uniform(ks[5], (D_OUT, D_OUT), jnp.float32, -s_out, s_out), 'b1': jax.random.uniform(ks[6], (D_OUT,), jnp.float32, -s_out, s_out), 'ln2_w': jnp.ones((D_OUT,), jnp.float32), 'ln2_b': jnp.zeros((D_OUT,), jnp.float32), 'W2': jax.random.uniform(ks[7], (D_OUT, D_OUT), jnp.float32, -s_out, s_out), 'b2': jax.random.uniform(ks[8], (D_OUT,), jnp.float32, -s_out, s_out), 'lnf_w': jnp.ones((D_OUT,), jnp.float32), 'lnf_b': jnp.zeros((D_OUT,), jnp.float32)}
    _L1_gnn_all = _L1_gnn_setup()
    _L1_gnn_in = {k: v for k, v in _L1_gnn_all.items() if k in ('Wq', 'Wk', 'Wv', 'ln1_w', 'ln1_b', 'W1', 'b1', 'ln2_w', 'ln2_b', 'W2', 'b2', 'lnf_w', 'lnf_b')}
    del _L1_gnn_all

    def _L2_gnn_setup():
        import jax, jax.numpy as jnp
        import numpy as np
        D_MODEL = 128
        NUM_REL = 40

        def _direction(x, W, Wg, b, bg, adj, rel_ids):
            h = x @ W.T
            g = h @ Wg.T
            vals = (h[:, :, None, :] + b) * jax.nn.sigmoid(g[:, :, None, :] + bg)
            onehot = (adj[..., None] == rel_ids).astype(h.dtype)
            return jnp.einsum('bnmr,bmrd->bnd', onehot, vals)
        key = jax.random.key(seed)
        ks = jax.random.split(key, 16)
        B, N, d = (2, 256, D_MODEL)
        s = 0.02
        inp = {'node': jax.random.normal(ks[0], (B, N, d), dtype=jnp.float32), 'node_mask': jnp.ones((B, N), dtype=jnp.float32), 'adj_mat': jax.random.randint(ks[1], (B, N, N), 0, 41, dtype=jnp.int32), 'W_fwd': jax.random.normal(ks[2], (d, d), dtype=jnp.float32) * s, 'W_bwd': jax.random.normal(ks[3], (d, d), dtype=jnp.float32) * s, 'W_loop': jax.random.normal(ks[4], (d, d), dtype=jnp.float32) * s, 'Wg_fwd': jax.random.normal(ks[5], (d, d), dtype=jnp.float32) * s, 'Wg_bwd': jax.random.normal(ks[6], (d, d), dtype=jnp.float32) * s, 'Wg_loop': jax.random.normal(ks[7], (d, d), dtype=jnp.float32) * s, 'b_fwd': jax.random.normal(ks[8], (NUM_REL - 1, d), dtype=jnp.float32) * s, 'b_bwd': jax.random.normal(ks[9], (NUM_REL - 1, d), dtype=jnp.float32) * s, 'b_loop': jax.random.normal(ks[10], (1, d), dtype=jnp.float32) * s, 'bg_fwd': jax.random.normal(ks[11], (NUM_REL - 1, d), dtype=jnp.float32) * s, 'bg_bwd': jax.random.normal(ks[12], (NUM_REL - 1, d), dtype=jnp.float32) * s, 'bg_loop': jax.random.normal(ks[13], (1, d), dtype=jnp.float32) * s}
        return inp
    _L2_gnn_all = _L2_gnn_setup()
    _L2_gnn_in = {k: v for k, v in _L2_gnn_all.items() if k in ('W_fwd', 'W_bwd', 'W_loop', 'Wg_fwd', 'Wg_bwd', 'Wg_loop', 'b_fwd', 'b_bwd', 'b_loop', 'bg_fwd', 'bg_bwd', 'bg_loop')}
    del _L2_gnn_all

    def _L3_gnn_setup():
        import jax, jax.numpy as jnp
        import numpy as np
        B, N, C_IN, H, C_OUT = (8, 512, 128, 4, 128)
        C = C_OUT // H
        ALPHA = 0.2
        NEG_INF = -9000000000000000.0
        key = jax.random.key(seed)
        k1, k2, k3, k4, k5 = jax.random.split(key, 5)
        node_feats = jax.random.normal(k1, (B, N, C_IN), dtype=jnp.float32)
        adj_matrix = jax.random.randint(k2, (B, N, N), 0, 2, dtype=jnp.int32)
        eye = jnp.eye(N, dtype=jnp.int32)[None]
        adj_matrix = jnp.maximum(adj_matrix, eye)

        def xavier(k, shape, fan_in, fan_out, gain=1.414):
            lim = gain * np.sqrt(6.0 / (fan_in + fan_out))
            return jax.random.uniform(k, shape, jnp.float32, -lim, lim)
        W = xavier(k3, (C_OUT, C_IN), C_IN, C_OUT)
        b = jnp.zeros((C_OUT,), dtype=jnp.float32)
        a = xavier(k4, (H, 2 * C), 2 * C, H)
        return {'node_feats': node_feats, 'adj_matrix': adj_matrix, 'W': W, 'b': b, 'a': a}
    _L3_gnn_all = _L3_gnn_setup()
    _L3_gnn_in = {k: v for k, v in _L3_gnn_all.items() if k in ('W', 'b', 'a')}
    del _L3_gnn_all
    return {'x': x, 'adj': adj, 'nodemask': nodemask, 'L0_gnn_W': _L0_gnn_in['W'], 'L0_gnn_a': _L0_gnn_in['a'], 'L1_gnn_Wq': _L1_gnn_in['Wq'], 'L1_gnn_Wk': _L1_gnn_in['Wk'], 'L1_gnn_Wv': _L1_gnn_in['Wv'], 'L1_gnn_ln1_w': _L1_gnn_in['ln1_w'], 'L1_gnn_ln1_b': _L1_gnn_in['ln1_b'], 'L1_gnn_W1': _L1_gnn_in['W1'], 'L1_gnn_b1': _L1_gnn_in['b1'], 'L1_gnn_ln2_w': _L1_gnn_in['ln2_w'], 'L1_gnn_ln2_b': _L1_gnn_in['ln2_b'], 'L1_gnn_W2': _L1_gnn_in['W2'], 'L1_gnn_b2': _L1_gnn_in['b2'], 'L1_gnn_lnf_w': _L1_gnn_in['lnf_w'], 'L1_gnn_lnf_b': _L1_gnn_in['lnf_b'], 'L2_gnn_W_fwd': _L2_gnn_in['W_fwd'], 'L2_gnn_W_bwd': _L2_gnn_in['W_bwd'], 'L2_gnn_W_loop': _L2_gnn_in['W_loop'], 'L2_gnn_Wg_fwd': _L2_gnn_in['Wg_fwd'], 'L2_gnn_Wg_bwd': _L2_gnn_in['Wg_bwd'], 'L2_gnn_Wg_loop': _L2_gnn_in['Wg_loop'], 'L2_gnn_b_fwd': _L2_gnn_in['b_fwd'], 'L2_gnn_b_bwd': _L2_gnn_in['b_bwd'], 'L2_gnn_b_loop': _L2_gnn_in['b_loop'], 'L2_gnn_bg_fwd': _L2_gnn_in['bg_fwd'], 'L2_gnn_bg_bwd': _L2_gnn_in['bg_bwd'], 'L2_gnn_bg_loop': _L2_gnn_in['bg_loop'], 'L3_gnn_W': _L3_gnn_in['W'], 'L3_gnn_b': _L3_gnn_in['b'], 'L3_gnn_a': _L3_gnn_in['a']}

def reference(x, adj, nodemask, L0_gnn_W, L0_gnn_a, L1_gnn_Wq, L1_gnn_Wk, L1_gnn_Wv, L1_gnn_ln1_w, L1_gnn_ln1_b, L1_gnn_W1, L1_gnn_b1, L1_gnn_ln2_w, L1_gnn_ln2_b, L1_gnn_W2, L1_gnn_b2, L1_gnn_lnf_w, L1_gnn_lnf_b, L2_gnn_W_fwd, L2_gnn_W_bwd, L2_gnn_W_loop, L2_gnn_Wg_fwd, L2_gnn_Wg_bwd, L2_gnn_Wg_loop, L2_gnn_b_fwd, L2_gnn_b_bwd, L2_gnn_b_loop, L2_gnn_bg_fwd, L2_gnn_bg_bwd, L2_gnn_bg_loop, L3_gnn_W, L3_gnn_b, L3_gnn_a):
    import jax
    import jax.numpy as jnp

    def _L0_gnn_ref(h, adj, W, a):
        import jax, jax.numpy as jnp
        import numpy as np
        IN_F = 128
        OUT_F = 128
        ALPHA = 0.2

        def _xavier(key, shape, gain=1.414):
            fan_in, fan_out = (shape[0], shape[1])
            limit = gain * np.sqrt(6.0 / (fan_in + fan_out))
            return jax.random.uniform(key, shape, jnp.float32, -limit, limit)
        Wh = jnp.einsum('bni,io->bno', h, W)
        a1 = a[:OUT_F, 0]
        a2 = a[OUT_F:, 0]
        e1 = Wh @ a1
        e2 = Wh @ a2
        e = e1[:, :, None] + e2[:, None, :]
        e = jnp.where(e > 0, e, ALPHA * e)
        neg = jnp.float32(-9000000000000000.0)
        scores = jnp.where(adj > 0, e, neg)
        attention = jax.nn.softmax(scores, axis=2)
        h_prime = jnp.einsum('bnm,bmo->bno', attention, Wh)
        return jax.nn.elu(h_prime)

    def _L1_gnn_ref(x, connectivity, Wq, Wk, Wv, ln1_w, ln1_b, W1, b1, ln2_w, ln2_b, W2, b2, lnf_w, lnf_b):
        import jax, jax.numpy as jnp
        import numpy as np
        EPS = 1e-05

        def _layernorm(x, w, b):
            m = jnp.mean(x, axis=-1, keepdims=True)
            v = jnp.mean((x - m) ** 2, axis=-1, keepdims=True)
            return (x - m) * jax.lax.rsqrt(v + EPS) * w + b

        def _swish(x):
            return x * jax.nn.sigmoid(x)
        D_OUT = Wq.shape[0]
        scale = jnp.sqrt(jnp.float32(D_OUT))
        Q = jnp.einsum('bah,oh->bao', x, Wq)
        K = jnp.einsum('bah,oh->bao', x, Wk)
        V = jnp.einsum('bah,oh->bao', x, Wv)
        scores = jnp.einsum('bqd,bkd->bqk', Q, K) / scale
        mask = (connectivity == 0).astype(scores.dtype) * -1000000000.0
        alpha = jax.nn.softmax(scores + mask, axis=-1)
        H = jnp.einsum('bqk,bkd->bqd', alpha, V)
        h = _layernorm(_swish(H), ln1_w, ln1_b)
        h = jnp.einsum('bad,od->bao', h, W1) + b1
        h = _layernorm(_swish(h), ln2_w, ln2_b)
        h = jnp.einsum('bad,od->bao', h, W2) + b2
        return _layernorm(h, lnf_w, lnf_b)

    def _L2_gnn_ref(node, node_mask, adj_mat, W_fwd, W_bwd, W_loop, Wg_fwd, Wg_bwd, Wg_loop, b_fwd, b_bwd, b_loop, bg_fwd, bg_bwd, bg_loop):
        import jax, jax.numpy as jnp
        import numpy as np
        D_MODEL = 128
        NUM_REL = 40

        def _direction(x, W, Wg, b, bg, adj, rel_ids):
            h = x @ W.T
            g = h @ Wg.T
            vals = (h[:, :, None, :] + b) * jax.nn.sigmoid(g[:, :, None, :] + bg)
            onehot = (adj[..., None] == rel_ids).astype(h.dtype)
            return jnp.einsum('bnmr,bmrd->bnd', onehot, vals)
        rels = jnp.arange(2, NUM_REL + 1, dtype=adj_mat.dtype)
        rel1 = jnp.array([1], dtype=adj_mat.dtype)
        adj_t = jnp.swapaxes(adj_mat, -1, -2)
        out = _direction(node, W_fwd, Wg_fwd, b_fwd, bg_fwd, adj_mat, rels)
        out = out + _direction(node, W_bwd, Wg_bwd, b_bwd, bg_bwd, adj_t, rels)
        out = out + _direction(node, W_loop, Wg_loop, b_loop, bg_loop, adj_t, rel1)
        return jax.nn.relu(out)

    def _L3_gnn_ref(node_feats, adj_matrix, W, b, a):
        import jax, jax.numpy as jnp
        import numpy as np
        B, N, C_IN, H, C_OUT = (8, 512, 128, 4, 128)
        C = C_OUT // H
        ALPHA = 0.2
        NEG_INF = -9000000000000000.0
        Bb, Nn, _ = node_feats.shape
        Hh, twoC = a.shape
        Cc = twoC // 2
        h = (node_feats @ W.T + b).reshape(Bb, Nn, Hh, Cc)
        a_src, a_dst = (a[:, :Cc], a[:, Cc:])
        l_src = jnp.einsum('bihc,hc->bih', h, a_src)
        l_dst = jnp.einsum('bjhc,hc->bjh', h, a_dst)
        logits = jax.nn.leaky_relu(l_src[:, :, None, :] + l_dst[:, None, :, :], ALPHA)
        logits = jnp.where(adj_matrix[..., None] == 1, logits, NEG_INF)
        probs = jax.nn.softmax(logits, axis=2)
        out = jnp.einsum('bijh,bjhc->bihc', probs, h)
        return out.reshape(Bb, Nn, Hh * Cc)
    x = _layernorm(x + _L0_gnn_ref(x, adj, L0_gnn_W, L0_gnn_a), axis=-1)
    x = _layernorm(x + _L1_gnn_ref(x, adj, L1_gnn_Wq, L1_gnn_Wk, L1_gnn_Wv, L1_gnn_ln1_w, L1_gnn_ln1_b, L1_gnn_W1, L1_gnn_b1, L1_gnn_ln2_w, L1_gnn_ln2_b, L1_gnn_W2, L1_gnn_b2, L1_gnn_lnf_w, L1_gnn_lnf_b), axis=-1)
    x = _layernorm(x + _L2_gnn_ref(x, nodemask, adj, L2_gnn_W_fwd, L2_gnn_W_bwd, L2_gnn_W_loop, L2_gnn_Wg_fwd, L2_gnn_Wg_bwd, L2_gnn_Wg_loop, L2_gnn_b_fwd, L2_gnn_b_bwd, L2_gnn_b_loop, L2_gnn_bg_fwd, L2_gnn_bg_bwd, L2_gnn_bg_loop), axis=-1)
    x = _layernorm(x + _L3_gnn_ref(x, adj, L3_gnn_W, L3_gnn_b, L3_gnn_a), axis=-1)
    return x

_drawn_inputs = setup_inputs


def setup_inputs(seed=0):
    import zlib

    import numpy as np

    out = dict(_drawn_inputs(seed))
    spreads = {'L1_gnn_ln1_w': (1.0, 0.2),
     'L1_gnn_ln1_b': (0.0, 0.1),
     'L1_gnn_ln2_w': (1.0, 0.2),
     'L1_gnn_ln2_b': (0.0, 0.1),
     'L1_gnn_lnf_w': (1.0, 0.2),
     'L1_gnn_lnf_b': (0.0, 0.1),
     'L3_gnn_b': (0.0, 0.1)}
    factors = {'L2_gnn_Wg_loop': 3.12, 'L2_gnn_bg_loop': 4.843}
    for name, (base, spread) in spreads.items():
        noise = np.random.default_rng([zlib.crc32(name.encode()), seed]).standard_normal(out[name].shape)
        drawn = base * np.exp(spread * noise) if base else spread * noise
        out[name] = jnp.asarray(drawn.astype(out[name].dtype))
    for name, factor in factors.items():
        out[name] = (out[name] * factor).astype(out[name].dtype)
    return out
```

```python
from contextlib import ExitStack

import numpy as np

import concourse.bass as bass
from concourse import mybir

P = 128
GRAPHS = 64
PER_GROUP = 4
CHAINS = 4
GROUPS = GRAPHS // PER_GROUP
ROUNDS = GROUPS // CHAINS
W = PER_GROUP * P
HEADS = 4
HEAD_C = P // HEADS
HS = HEAD_C + 1
ALPHA = 0.2
EPS = 1e-5
NEG_GAT = float(2.0 ** 53)
NEG_ATT = float(2.0 ** 30)

F32 = mybir.dt.float32
BF16 = mybir.dt.bfloat16
I32 = mybir.dt.int32
ALU = mybir.AluOpType
ACT = mybir.ActivationFunctionType
AX_X = mybir.AxisListType.X

WEIGHTS = ["W0", "W0T", "Wq", "Wk", "WvT", "W1T", "W2T", "Wl", "WlT", "WgT", "W3", "W3T"]
COLUMNS = ["a0_src", "a0_dst", "ln1_w", "ln1_b", "ln2_w", "ln2_b", "a3_src", "a3_dst", "b3"]
ROWS = ["b1", "b2", "b_loop", "bg_loop", "b3", "lnf_w", "lnf_b"]
VECTORS = ["s1", "s2", "src0", "dst0", "src3", "dst3", "b_s1", "b_s2", "b_keep"]
CONSTS = P + HEADS + 2 * W + len(VECTORS)
BIASES = 5


def constants():
    c = np.zeros((P, CONSTS), np.float32)
    c[:, :P] = np.eye(P)
    for h in range(HEADS):
        c[h * HEAD_C:(h + 1) * HEAD_C, P + h] = 1
    sel0 = c[:, P + HEADS:P + HEADS + W].reshape(P, PER_GROUP, P)
    sel3 = c[:, P + HEADS + W:P + HEADS + 2 * W].reshape(P, HEADS, P)
    vec = {name: c[:, P + HEADS + 2 * W + k] for k, name in enumerate(VECTORS)}
    for p in range(P):
        g, slot = divmod(p, 32)
        if slot < 24:
            sel3[p, slot % HEADS] = 1
            vec["src3" if slot < 12 else "dst3"][p] = 1
        if slot < 6:
            sel0[p, g] = 1
            vec["src0" if slot < 3 else "dst0"][p] = 1
    for p in range(3):
        vec["b_keep"][p] = 1
        vec["b_s1"][p] = -1.0 if p else 0.0
        vec["b_s2"][p] = -1.0 if p == 2 else 0.0
    return c


def split_vectors():
    s = np.zeros((P, 4), np.float32)
    for p in range(P):
        slot = p % 32
        if slot < 6:
            s[p, 0] = -1.0 if slot % 3 else 0.0
            s[p, 1] = -1.0 if slot % 3 == 2 else 0.0
        if slot < 24:
            part = (slot % 12) // HEADS
            s[p, 2] = -1.0 if part else 0.0
            s[p, 3] = -1.0 if part == 2 else 0.0
    return s


def graph_layers_kernel(nc, x_d, adj_d, w_d, col_d, row_d, const_d, split_d, out_d):
    with ExitStack() as ctx:
        def sb(name, shape, dt=F32):
            return ctx.enter_context(nc.sbuf_tensor(name, shape, dt))

        def chain_tiles(name, shape, dt=F32):
            return [sb(f"{name}{c}", shape, dt) for c in range(CHAINS)]

        def sem(name):
            return ctx.enter_context(nc.semaphore(name))

        bank_a = [ctx.enter_context(nc.psum_tensor(f"bank_a{c}", [P, W], F32)) for c in range(CHAINS)]
        bank_b = [ctx.enter_context(nc.psum_tensor(f"bank_b{c}", [P, W], F32)) for c in range(CHAINS)]

        wts = sb("wts", [P, len(WEIGHTS), P])
        cols = sb("cols", [P, len(COLUMNS)])
        rows = sb("rows", [P, len(ROWS), P])
        cst = sb("cst", [P, CONSTS])
        spl = sb("spl", [P, 4])
        qk = sb("qk", [P, P])
        w1a = sb("w1a", [P, P])
        w2a = sb("w2a", [P, P])
        gate = sb("gate", [P, P])
        a0s = sb("a0s", [P, 32])
        a3s = sb("a3s", [P, PER_GROUP, 32])
        slots0 = sb("slots0", [P, PER_GROUP, P])
        slots3 = sb("slots3", [P, PER_GROUP, P])
        kz3 = sb("kz3", [P, 1])
        ln_b_wide = sb("ln_b_wide", [P, 2, P])
        bias_f = sb("bias_f", [P, BIASES, P])
        bias_h = sb("bias_h", [P, BIASES, P], BF16)
        bias_r = sb("bias_r", [P, BIASES, P])
        bias_l = sb("bias_l", [P, BIASES, P])
        bias_parts = sb("bias_parts", [P, BIASES, P], BF16)
        ones_h = sb("ones_h", [P, P], BF16)
        ones_col = sb("ones_col", [P, 1])
        big_gat = sb("big_gat", [P, P], BF16)
        big_att = sb("big_att", [P, P], BF16)
        sel0 = sb("sel0", [P, PER_GROUP, P], BF16)
        sel3 = sb("sel3", [P, HEADS, P], BF16)
        half_pow = sb("half_pow", [P, PER_GROUP])

        def wt(name):
            return wts[:, WEIGHTS.index(name), :]

        def col(name):
            k = COLUMNS.index(name)
            return cols[:, k:k + 1]

        def row(name):
            return rows[:, ROWS.index(name), :]

        def vec(name):
            k = P + HEADS + 2 * W + VECTORS.index(name)
            return cst[:, k:k + 1]

        ident = cst[:, 0:P]
        head_of = cst[:, P:P + HEADS]

        x0 = chain_tiles("x0", [P, PER_GROUP, P])
        adj = chain_tiles("adj", [P, PER_GROUP, P], I32)
        x1 = chain_tiles("x1", [P, PER_GROUP, P])
        x2 = chain_tiles("x2", [P, PER_GROUP, P])
        x3 = chain_tiles("x3", [P, PER_GROUP, P])
        xo = chain_tiles("xo", [P, PER_GROUP, P])
        xb = chain_tiles("xb", [P, PER_GROUP, P])
        xT = chain_tiles("xT", [P, PER_GROUP, P])
        val = chain_tiles("val", [P, PER_GROUP, P])
        qT = chain_tiles("qT", [P, PER_GROUP, P])
        sc = chain_tiles("sc", [P, PER_GROUP, P])
        pr = chain_tiles("pr", [P, PER_GROUP, P])
        pT = chain_tiles("pT", [P, PER_GROUP, P])
        t1 = chain_tiles("t1", [P, PER_GROUP, P])
        t2 = chain_tiles("t2", [P, PER_GROUP, P])
        h3 = chain_tiles("h3", [P, PER_GROUP, HEADS, HS])
        pos_m1 = chain_tiles("pos_m1", [P, PER_GROUP, P], BF16)
        zero_m = chain_tiles("zero_m", [P, PER_GROUP, P], BF16)
        one_m1 = chain_tiles("one_m1", [P, PER_GROUP, P], BF16)
        one_half = chain_tiles("one_half", [P, PER_GROUP, P])
        e_f = chain_tiles("e_f", [P, P])
        e_h = chain_tiles("e_h", [P, P], BF16)
        e_r = chain_tiles("e_r", [P, P])
        e_h2 = chain_tiles("e_h2", [P, P], BF16)
        e_parts = chain_tiles("e_parts", [P, P], BF16)
        e_lhs = chain_tiles("e_lhs", [P, P], BF16)
        e_row = chain_tiles("e_row", [P, P], BF16)
        e_rhs = chain_tiles("e_rhs", [P, 4, P], BF16)
        nmax = chain_tiles("nmax", [P, PER_GROUP])
        rsum = chain_tiles("rsum", [P, PER_GROUP])
        stats = chain_tiles("stats", [P, 2, 2, 3])
        veps = chain_tiles("veps", [P, PER_GROUP])
        rstd = chain_tiles("rstd", [P, PER_GROUP])

        def per_graph(tile):
            return tile[:, :].unsqueeze(2).broadcast_to([P, PER_GROUP, P])

        def mean_of(c, g):
            return stats[c][:, g // 2, g % 2, 1:2]

        params_loaded = sem("params_loaded")
        x_loaded = [sem(f"x_loaded{c}") for c in range(CHAINS)]
        adj_loaded = [sem(f"adj_loaded{c}") for c in range(CHAINS)]
        stored = [sem(f"stored{c}") for c in range(CHAINS)]
        names = """h_z h_relu l0_relu prep_step prep_pe prep_pow
            pos_mask masks
            l0_xTp l0_xT l0_ep l0_valp l0_val l0_ef l0_z
            l1_xTp l1_xT l1_qTp l1_qT l1_sp l1_valp l1_val l1_shift
            n1_xTp n1_xT n1_hp n1_th n2_xTp n2_xT n2_hp xb_ready n3_scaled n3_w
            l2_xTp l2_xT l2_hp l2_gp l2_th l2_v l2_out l2_res
            l3_xTp l3_xT l3_ep l3_hp l3_h l3_ef l3_out l3_res
            h_leaky h_max h_sub h_exp h_pTp h_pT h_pv h_rs h_out""".split()
        for layer in ("l0", "l3"):
            names += [f"{layer}_{s}" for s in ("eh", "er", "eh2", "parts", "lhs", "row", "rhs")]
        for layer in ("l0", "l1"):
            names += [f"{layer}_{s}" for s in ("leaky", "max", "sub", "exp", "pTp", "pT", "pv", "rs", "h", "act", "gated", "res")]
        for norm in ("na", "nb", "nc", "nd", "ne", "nf", "ng"):
            names += [f"{norm}_{s}" for s in ("stats", "veps", "rstd", "x")]
        S = {name: sem(name) for name in names}

        block = ctx.enter_context(nc.Block())

        @block.sync
        def _(sp):
            for dst, src in ((cst, const_d), (wts, w_d), (cols, col_d), (spl, split_d), (rows, row_d)):
                sp.dma_start(dst[:], src).then_inc(params_loaded, 16)
            with sp.Fori(0, ROUNDS) as r:
                done = [sp.to_reg(r * CHAINS + (c + 1)) for c in range(CHAINS)]
                for c in range(CHAINS):

                    sp.dma_start(x0[c][:], x_d[:, bass.ds(r * (CHAINS * PER_GROUP) + c * PER_GROUP, PER_GROUP), :]).then_inc(x_loaded[c], 16)
                    sp.dma_start(adj[c][:], adj_d[:, bass.ds(r * (CHAINS * PER_GROUP) + c * PER_GROUP, PER_GROUP), :]).then_inc(adj_loaded[c], 16)
                for c in range(CHAINS):
                    sp.wait_ge(params_loaded, 16 * 5)
                    sp.wait_ge(S["l0_res"], done[c])
                    sp.wait_ge(S["masks"], done[c])

        prepared = {}

        @block.vector
        def _(dve):
            steps = [0]

            def prep(ins):
                steps[0] += 1
                ins.then_inc(S["prep_step"], 1)
                dve.wait_ge(S["prep_step"], steps[0])

            v = nc.vector
            dve.wait_ge(params_loaded, 16 * 5)
            prep(v.memset(a0s[:], 0.0))
            prep(v.memset(a3s[:], 0.0))
            prep(v.memset(slots0[:], 0.0))
            prep(v.memset(slots3[:], 0.0))
            prep(v.memset(ones_h[:], 1.0))
            prep(v.memset(ones_col[:], 1.0))
            for c in range(CHAINS):
                prep(v.memset(h3[c][:, :, :, HEAD_C:HS], 1.0))
            for part in range(3):
                prep(v.tensor_copy(a0s[:, part:part + 1], col("a0_src")))
                prep(v.tensor_copy(a0s[:, 3 + part:4 + part], col("a0_dst")))
                for g in range(PER_GROUP):
                    prep(v.tensor_scalar(a3s[:, g, 4 * part:4 * part + 4], head_of, col("a3_src"), None, ALU.mult))
                    prep(v.tensor_scalar(a3s[:, g, 12 + 4 * part:16 + 4 * part], head_of, col("a3_dst"), None, ALU.mult))
            prep(v.tensor_scalar(w1a[:], wt("W1T"), col("ln1_w"), None, ALU.mult))
            prep(v.tensor_scalar(w2a[:], wt("W2T"), col("ln2_w"), None, ALU.mult))
            prep(v.tensor_copy(ln_b_wide[:, 0, :], col("ln1_b").broadcast_to([P, P])))
            prep(v.tensor_copy(ln_b_wide[:, 1, :], col("ln2_b").broadcast_to([P, P])))
            prep(v.tensor_scalar(big_gat[:], ident, NEG_GAT, None, ALU.mult))
            prep(v.tensor_scalar(big_att[:], ident, NEG_ATT, None, ALU.mult))
            prep(v.tensor_copy(sel0[:], cst[:, P + HEADS:P + HEADS + W].rearrange("p (a k) -> p a k", a=4)))
            prep(v.tensor_copy(sel3[:], cst[:, P + HEADS + W:P + HEADS + 2 * W].rearrange("p (a k) -> p a k", a=4)))
            prep(v.tensor_copy(bias_f[:, 2:5, :], rows[:, 2:5, :]))
            prepared["operands"] = steps[0]
            dve.wait_ge(S["prep_pe"], 1)
            prep(v.tensor_scalar(qk[:], bank_a[0][:, 0:P], float(P) ** -0.5, None, ALU.mult))
            prep(v.tensor_copy(gate[:], bank_a[0][:, P:2 * P]))
            for k, b in enumerate(("b1", "b2")):
                prep(v.tensor_tensor(bias_f[:, k, :], bank_a[0][:, (2 + k) * P:(3 + k) * P], row(b), ALU.add))
            for g in range(PER_GROUP):
                prep(v.tensor_copy(slots0[:, g, 32 * g:32 * g + 32], bank_b[0][:, 0:32]))
                prep(v.tensor_copy(slots3[:, g, 32 * g:32 * g + 32], bank_b[0][:, 32:64]))
            prep(v.tensor_copy(kz3[:], bank_b[0][:, 64:65]))
            prep(v.tensor_copy(bias_h[:], bias_f[:]))
            prep(v.scalar_tensor_tensor(bias_r[:], bias_h[:], vec("b_s1"), bias_f[:], ALU.mult, ALU.add))
            prep(v.tensor_copy(bias_h[:], bias_r[:]))
            prep(v.scalar_tensor_tensor(bias_l[:], bias_h[:], vec("b_s2"), bias_r[:], ALU.mult, ALU.add))
            prep(v.tensor_scalar(bias_parts[:], bias_l[:], vec("b_keep"), None, ALU.mult))
            prepared["all"] = steps[0]

            with dve.Fori(0, ROUNDS) as r:
                done = [dve.snap(r * CHAINS + (c + 1)) for c in range(CHAINS)]

                def a_bank(c):
                    return bank_a[c][:, :].rearrange("p (g k) -> p g k", g=PER_GROUP)

                def b_bank(c):
                    return bank_b[c][:, :].rearrange("p (g k) -> p g k", g=PER_GROUP)

                def every(name, after, op):
                    for c in range(CHAINS):
                        for s in after:
                            dve.wait_ge(S[s], done[c])
                        op(c).then_inc(S[name], 1)

                def split(layer, s, src, dst):
                    every(f"{layer}_eh", [f"{layer}_ef"], lambda c: v.tensor_copy(e_h[c][:], e_f[c][:]))
                    every(f"{layer}_er", [f"{layer}_eh"], lambda c: v.scalar_tensor_tensor(
                        e_r[c][:], e_h[c][:], spl[:, s:s + 1], e_f[c][:], ALU.mult, ALU.add))
                    every(f"{layer}_eh2", [f"{layer}_er"], lambda c: v.tensor_copy(e_h2[c][:], e_r[c][:]))
                    every(f"{layer}_parts", [f"{layer}_eh2"], lambda c: v.scalar_tensor_tensor(
                        e_parts[c][:], e_h2[c][:], spl[:, s + 1:s + 2], e_r[c][:], ALU.mult, ALU.add))
                    every(f"{layer}_row", [f"{layer}_parts"], lambda c: v.tensor_scalar(
                        e_row[c][:], e_parts[c][:], vec(dst), vec(src), ALU.mult, ALU.add))
                    every(f"{layer}_lhs", [f"{layer}_parts"], lambda c: v.tensor_scalar(
                        e_lhs[c][:], e_parts[c][:], vec(src), vec(dst), ALU.mult, ALU.add))

                def statistics(norm, after, src):
                    for c in range(CHAINS):
                        dve.wait_ge(S[after], done[c])
                        for k in range(2):
                            last = v.bn_stats(stats[c][:, k, :, :].rearrange("p a s -> p (a s)"),
                                              src(c)[:, 2 * k:2 * k + 2, :].rearrange("p g k -> p k g"))
                        last.then_inc(S[norm + "_stats"], 1)

                every("l0_val", ["l0_valp"], lambda c: v.tensor_scalar(val[c][:], b_bank(c), 1.0, None, ALU.add))
                split("l0", 0, "src0", "dst0")
                every("l0_leaky", ["l0_relu"], lambda c: v.tensor_tensor(sc[c][:], a_bank(c), sc[c][:], ALU.add))
                every("l0_max", ["l0_leaky"], lambda c: v.tensor_reduce(nmax[c][:], sc[c][:], AX_X, ALU.max, negate=True))
                every("l0_rs", ["l0_pv"], lambda c: v.reciprocal(rsum[c][:], bank_a[c][:, 0:PER_GROUP]))
                every("l0_h", ["l0_rs"], lambda c: v.tensor_tensor(t1[c][:], b_bank(c), per_graph(rsum[c]), ALU.mult))
                every("l0_gated", ["l0_act"], lambda c: v.scalar_tensor_tensor(
                    t2[c][:], t2[c][:], 1.0, t1[c][:], ALU.min, ALU.max))
                statistics("na", "l0_res", lambda c: t2[c])
                every("l1_qT", ["l1_qTp"], lambda c: v.tensor_copy(qT[c][:], b_bank(c)))
                every("l1_max", ["l1_sp"], lambda c: v.tensor_reduce(nmax[c][:], a_bank(c), AX_X, ALU.max, negate=True))
                every("l1_sub", ["l1_max"], lambda c: v.tensor_tensor(sc[c][:], a_bank(c), per_graph(nmax[c]), ALU.add))
                every("l1_rs", ["l1_pv"], lambda c: v.reciprocal(rsum[c][:], bank_a[c][:, 0:PER_GROUP]))
                every("l1_h", ["l1_rs"], lambda c: v.tensor_tensor(t1[c][:], b_bank(c), per_graph(rsum[c]), ALU.mult))
                every("l1_gated", ["l1_act"], lambda c: v.scalar_tensor_tensor(
                    t1[c][:], t2[c][:], 1.0, t1[c][:], ALU.add, ALU.mult))
                statistics("nb", "l1_gated", lambda c: t1[c])
                every("l1_leaky", ["n1_th"], lambda c: v.scalar_tensor_tensor(
                    t2[c][:], t1[c][:], 1.0, b_bank(c), ALU.add, ALU.mult))
                statistics("nc", "l1_leaky", lambda c: t2[c])
                statistics("nd", "n2_hp", b_bank)
                for c in range(CHAINS):
                    dve.wait_ge(S["nd_rstd"], done[c])
                    for g in range(PER_GROUP):
                        last = v.tensor_scalar(t1[c][:, g, :], bank_b[c][:, g * P:(g + 1) * P], mean_of(c, g),
                                               rstd[c][:, g:g + 1], ALU.subtract, ALU.mult)
                    last.then_inc(S["nd_x"], 1)
                statistics("ne", "l1_res", lambda c: t2[c])
                every("l2_v", ["l2_th", "l2_hp"], lambda c: v.scalar_tensor_tensor(
                    t2[c][:], t1[c][:], 1.0, b_bank(c), ALU.add, ALU.mult))
                every("l2_res", ["l2_out"], lambda c: v.scalar_tensor_tensor(
                    t1[c][:], b_bank(c), 0.0, x2[c][:], ALU.max, ALU.add))
                statistics("nf", "l2_res", lambda c: t1[c])
                split("l3", 2, "src3", "dst3")
                done4 = [dve.snap(r * (CHAINS * PER_GROUP) + (c + 1)) for c in range(CHAINS * PER_GROUP)]
                for g in range(PER_GROUP):
                    for c in range(CHAINS):
                        dve.wait_ge(S["h_relu"], done4[g * CHAINS + c])
                        v.tensor_tensor(sc[c][:], a_bank(c), sc[c][:], ALU.add).then_inc(S["h_leaky"], 1)
                    for c in range(CHAINS):
                        dve.wait_ge(S["h_leaky"], done4[g * CHAINS + c])
                        v.tensor_reduce(nmax[c][:], sc[c][:], AX_X, ALU.max, negate=True).then_inc(S["h_max"], 1)
                    for c in range(CHAINS):
                        dve.wait_ge(S["h_pTp"], done4[g * CHAINS + c])
                        v.tensor_copy(pT[c][:], a_bank(c)).then_inc(S["h_pT"], 1)
                    heads = [bank_b[c][:, 0:HEADS * HS].rearrange("p (h k) -> p h k", h=HEADS) for c in range(CHAINS)]
                    for c in range(CHAINS):
                        dve.wait_ge(S["h_pv"], done4[g * CHAINS + c])
                        v.reciprocal(rsum[c][:].unsqueeze(2), heads[c][:, :, HEAD_C:HS]).then_inc(S["h_rs"], 1)
                    for c in range(CHAINS):
                        dve.wait_ge(S["h_rs"], done4[g * CHAINS + c])
                        v.tensor_tensor(t1[c][:, g, :].rearrange("p (h k) -> p h k", h=HEADS), heads[c][:, :, 0:HEAD_C],
                                        rsum[c][:].unsqueeze(2).broadcast_to([P, HEADS, HEAD_C]), ALU.mult).then_inc(S["h_out"], 1)
                statistics("ng", "l3_res", lambda c: t1[c])

        @block.gpsimd
        def _(pool):
            pool.memset(half_pow[:], -0.5).then_inc(S["prep_pow"], 1)
            pool.wait_ge(S["prep_pow"], 1)
            with pool.Fori(0, ROUNDS) as r:
                done = [pool.snap(r * CHAINS + (c + 1)) for c in range(CHAINS)]

                def settle():
                    pool.wait_ge(S["prep_pow"], 1)

                def spread(name, after, c, e, selector):
                    pool.wait_ge(S[after], done[c])
                    nc.gpsimd.tensor_tensor(e_rhs[c][:], e_row[c][:].unsqueeze(1).broadcast_to([P, 4, P]), selector[:],
                                            ALU.mult).then_inc(S[name], 1)

                def rstd_of(norm, scale, eps):
                    for c in range(CHAINS):
                        settle()
                        pool.wait_ge(S[norm + "_stats"], done[c])
                        nc.gpsimd.tensor_scalar(veps[c][:], stats[c][:, :, :, 2:3].rearrange("p a b o -> p (a b o)"),
                                                scale, eps, ALU.mult, ALU.add).then_inc(S[norm + "_veps"], 1)
                    for c in range(CHAINS):
                        pool.wait_ge(S[norm + "_veps"], done[c])
                        nc.gpsimd.tensor_tensor(rstd[c][:], veps[c][:], half_pow[:], ALU.pow).then_inc(S[norm + "_rstd"], 1)

                def normalise(norm, src, dst):
                    for c in range(CHAINS):
                        settle()
                        pool.wait_ge(S[norm + "_rstd"], done[c])
                        for g in range(PER_GROUP):
                            last = nc.gpsimd.tensor_scalar(dst[c][:, g, :], src[c][:, g, :], mean_of(c, g),
                                                           rstd[c][:, g:g + 1], ALU.subtract, ALU.mult)
                        last.then_inc(S[norm + "_x"], 1)

                loaded = pool.to_reg(r * 16 + 16)
                for c in range(CHAINS):
                    settle()
                    pool.wait_ge(adj_loaded[c], loaded)
                    nc.gpsimd.tensor_scalar(pos_m1[c][:], adj[c][:], 0.0, -1.0, ALU.is_gt, ALU.add).then_inc(S["pos_mask"], 1)
                for c in range(CHAINS):
                    spread("l0_rhs", "l0_row", c, e_rhs, sel0)
                for c in range(CHAINS):
                    nc.gpsimd.tensor_scalar(zero_m[c][:], adj[c][:], 0.0, -1.0, ALU.is_equal, ALU.mult)
                    nc.gpsimd.tensor_scalar(one_half[c][:], adj[c][:], 1.0, 0.5, ALU.is_equal, ALU.mult)
                    nc.gpsimd.tensor_scalar(one_m1[c][:], adj[c][:], 1.0, -1.0, ALU.is_equal, ALU.add).then_inc(S["masks"], 1)
                for c in range(CHAINS):
                    pool.wait_ge(S["l0_max"], done[c])
                    nc.gpsimd.tensor_tensor(sc[c][:], sc[c][:], per_graph(nmax[c]), ALU.add).then_inc(S["l0_sub"], 1)
                for c in range(CHAINS):
                    pool.wait_ge(S["l0_gated"], done[c])
                    nc.gpsimd.tensor_tensor(t2[c][:], t2[c][:], x0[c][:], ALU.add).then_inc(S["l0_res"], 1)
                rstd_of("na", 1.0 / P, EPS)
                normalise("na", t2, x1)
                for c in range(CHAINS):
                    pool.wait_ge(S["na_x"], done[c])
                    nc.gpsimd.tensor_tensor(xb[c][:], x1[c][:], row("lnf_b").unsqueeze(1).broadcast_to([P, PER_GROUP, P]),
                                            ALU.add).then_inc(S["xb_ready"], 1)
                rstd_of("nb", 1.0 / P, 4 * EPS)
                normalise("nb", t1, t2)
                rstd_of("nc", 1.0 / P, 4 * EPS)
                normalise("nc", t2, t1)
                rstd_of("nd", 1.0 / P, EPS)
                for c in range(CHAINS):
                    pool.wait_ge(S["nd_x"], done[c])
                    nc.gpsimd.tensor_tensor(t1[c][:], t1[c][:], row("lnf_w").unsqueeze(1).broadcast_to([P, PER_GROUP, P]),
                                            ALU.mult).then_inc(S["n3_w"], 1)
                for c in range(CHAINS):
                    pool.wait_ge(S["n3_w"], done[c])
                    nc.gpsimd.tensor_tensor(t2[c][:], t1[c][:], xb[c][:], ALU.add).then_inc(S["l1_res"], 1)
                rstd_of("ne", 1.0 / P, EPS)
                normalise("ne", t2, x2)
                rstd_of("nf", 1.0 / P, EPS)
                normalise("nf", t1, x3)
                for c in range(CHAINS):
                    spread("l3_rhs", "l3_row", c, e_rhs, sel3)
                done4 = [pool.snap(r * (CHAINS * PER_GROUP) + (c + 1)) for c in range(CHAINS * PER_GROUP)]
                for g in range(PER_GROUP):
                    for c in range(CHAINS):
                        pool.wait_ge(S["h_max"], done4[g * CHAINS + c])
                        nc.gpsimd.tensor_tensor(sc[c][:], sc[c][:], per_graph(nmax[c]), ALU.add).then_inc(S["h_sub"], 1)
                for c in range(CHAINS):
                    pool.wait_ge(S["h_out"], done4[(PER_GROUP - 1) * CHAINS + c])
                    nc.gpsimd.tensor_tensor(t1[c][:], t1[c][:], x3[c][:], ALU.add).then_inc(S["l3_res"], 1)
                rstd_of("ng", 1.0 / P, EPS)
                for c in range(CHAINS):
                    settle()
                    pool.wait_ge(S["ng_rstd"], done[c])
                    for g in range(PER_GROUP):
                        last = nc.gpsimd.tensor_scalar(xo[c][:, g, :], t1[c][:, g, :], mean_of(c, g),
                                                       rstd[c][:, g:g + 1], ALU.subtract, ALU.mult)
                    last.then_inc(S["ng_x"], 1)
                for c in range(CHAINS):
                    pool.wait_ge(S["ng_x"], done[c])
                    pool.dma_start(out_d[:, bass.ds(r * (CHAINS * PER_GROUP) + c * PER_GROUP, PER_GROUP), :], xo[c][:]).then_inc(stored[c], 16)
                for c in range(CHAINS):
                    pool.wait_ge(stored[c], loaded)

        @block.scalar
        def _(act):
            act.wait_ge(S["prep_step"], prepared["all"])
            with act.Fori(0, ROUNDS) as r:
                done = [act.snap(r * CHAINS + (c + 1)) for c in range(CHAINS)]

                def move(name, after, dst, bank, func=ACT.Copy, **kw):
                    for c in range(CHAINS):
                        act.wait_ge(S[after], done[c])
                        nc.scalar.activation(dst(c), bank(c), func, **kw).then_inc(S[name], 1)

                def a_bank(c):
                    return bank_a[c][:, :].rearrange("p (g k) -> p g k", g=PER_GROUP)

                def b_bank(c):
                    return bank_b[c][:, :].rearrange("p (g k) -> p g k", g=PER_GROUP)

                move("l0_xT", "l0_xTp", lambda c: xT[c][:], a_bank)
                move("l0_ef", "l0_ep", lambda c: e_f[c][:], lambda c: bank_a[c][:, 0:P])
                move("l0_relu", "l0_z", lambda c: sc[c][:], a_bank, ACT.Relu, scale=1 / ALPHA - 1)
                move("l0_exp", "l0_sub", lambda c: pr[c][:], lambda c: sc[c][:], ACT.Exp, scale=ALPHA)
                move("l0_pT", "l0_pTp", lambda c: pT[c][:], a_bank)
                move("l0_act", "l0_h", lambda c: t2[c][:], lambda c: t1[c][:], ACT.Exp, bias=-1.0)
                move("l1_xT", "l1_xTp", lambda c: xT[c][:], a_bank)
                move("l1_val", "l1_valp", lambda c: val[c][:], b_bank)
                move("l1_exp", "l1_sub", lambda c: pr[c][:], lambda c: sc[c][:], ACT.Exp)
                move("l1_pT", "l1_pTp", lambda c: pT[c][:], a_bank)
                move("l1_act", "l1_h", lambda c: t2[c][:], lambda c: t1[c][:], ACT.Tanh, scale=0.5)
                move("n1_xT", "n1_xTp", lambda c: xT[c][:], a_bank)
                move("n1_th", "n1_hp", lambda c: t1[c][:], b_bank, ACT.Tanh, scale=0.5)
                move("n2_xT", "n2_xTp", lambda c: xT[c][:], a_bank)
                move("l2_xT", "l2_xTp", lambda c: xT[c][:], a_bank)
                move("l2_th", "l2_gp", lambda c: t1[c][:], a_bank, ACT.Tanh, scale=0.5)
                move("l3_xT", "l3_xTp", lambda c: xT[c][:], a_bank)
                move("l3_ef", "l3_ep", lambda c: e_f[c][:], lambda c: bank_a[c][:, 0:P], ACT.Identity, bias=kz3[:, 0:1])
                move("l3_h", "l3_hp", lambda c: h3[c][:, :, :, 0:HEAD_C],
                     lambda c: bank_b[c][:, :].rearrange("p (g h k) -> p g h k", g=PER_GROUP, h=HEADS))
                done4 = [act.snap(r * (CHAINS * PER_GROUP) + (c + 1)) for c in range(CHAINS * PER_GROUP)]
                for g in range(PER_GROUP):
                    for c in range(CHAINS):
                        act.wait_ge(S["h_z"], done4[g * CHAINS + c])
                        nc.scalar.activation(sc[c][:], a_bank(c), ACT.Relu, scale=1 / ALPHA - 1).then_inc(S["h_relu"], 1)
                    for c in range(CHAINS):
                        act.wait_ge(S["h_sub"], done4[g * CHAINS + c])
                        nc.scalar.activation(pr[c][:], sc[c][:], ACT.Exp, scale=ALPHA).then_inc(S["h_exp"], 1)

        @block.tensor
        def _(pe):
            t = nc.tensor
            pe.wait_ge(params_loaded, 16 * 5)
            pe.wait_ge(S["prep_step"], prepared["operands"])
            t.matmul(bank_a[0][:, 0:P], wt("Wq"), wt("Wk"), start=True, stop=True)
            t.matmul(bank_a[0][:, P:2 * P], wt("Wl"), wt("WgT"), start=True, stop=True)
            t.matmul(bank_a[0][:, 2 * P:3 * P], ln_b_wide[:, 0, :], wt("W1T"), start=True, stop=True)
            t.matmul(bank_a[0][:, 3 * P:4 * P], ln_b_wide[:, 1, :], wt("W2T"), start=True, stop=True)
            t.matmul(bank_b[0][:, 0:32], wt("W0T"), a0s[:], start=True, stop=True)
            t.matmul(bank_b[0][:, 32:64], wt("W3"), a3s[:, 0, :], start=True, stop=True)
            t.matmul(bank_b[0][:, 64:65], a3s[:].rearrange("p g s -> p (g s)"), col("b3"),
                     start=True, stop=True).then_inc(S["prep_pe"], 1)
            pe.wait_ge(S["prep_step"], prepared["all"])
            with pe.Fori(0, ROUNDS) as r:
                done = [pe.snap(r * CHAINS + (c + 1)) for c in range(CHAINS)]
                loaded = pe.snap(r * 16 + 16)

                def cut(bank, g):
                    return bank[:, g * P:(g + 1) * P]

                def transposes(name, after, src):
                    for c in range(CHAINS):
                        for s in after:
                            pe.wait_ge(s, done[c]) if not isinstance(s, str) else pe.wait_ge(S[s], done[c])
                        for g in range(PER_GROUP):
                            last = t.transpose(cut(bank_a[c], g), src[c][:, g, :], ident)
                        last.then_inc(S[name], 1)

                def project(name, after, bank, weights, bias=None):
                    for c in range(CHAINS):
                        for s in after:
                            pe.wait_ge(S[s], done[c])
                        if bias is not None:
                            t.matmul(bank[c][:, :].rearrange("p (g k) -> p g k", g=PER_GROUP), ones_h[:],
                                     bias_parts[:, bias, :].unsqueeze(1).broadcast_to([P, PER_GROUP, P]),
                                     start=True, stop=False, skip_group_check=True)
                        for g in range(PER_GROUP):
                            last = t.matmul(cut(bank[c], g), xT[c][:, g, :], weights, start=bias is None and g == 0,
                                            stop=g == PER_GROUP - 1, skip_group_check=True)
                        last.then_inc(S[name], 1)

                def logits(name, after, slots):
                    for c in range(CHAINS):
                        for s in after:
                            pe.wait_ge(S[s], done[c])
                        for g in range(PER_GROUP):
                            last = t.matmul(bank_a[c][:, 0:P], slots[:, g, :], xT[c][:, g, :], start=g == 0, stop=g == PER_GROUP - 1)
                        last.then_inc(S[name], 1)

                def attend(layer):
                    for c in range(CHAINS):
                        pe.wait_ge(S[layer + "_pT"], done[c])
                        pe.wait_ge(S[layer + "_val"], done[c])
                        for g in range(PER_GROUP):
                            t.matmul(cut(bank_b[c], g), pT[c][:, g, :], val[c][:, g, :], start=True, stop=True)
                        for g in range(PER_GROUP):
                            last = t.matmul(bank_a[c][:, g:g + 1], pT[c][:, g, :], ones_col[:], start=True, stop=True)
                        last.then_inc(S[layer + "_pv"], 1)

                for c in range(CHAINS):
                    pe.wait_ge(x_loaded[c], loaded)
                    for g in range(PER_GROUP):
                        last = t.transpose(cut(bank_a[c], g), x0[c][:, g, :], ident)
                    last.then_inc(S["l0_xTp"], 1)
                logits("l0_ep", ["l0_xT"], slots0)
                project("l0_valp", [], bank_b, wt("W0"))
                for c in range(CHAINS):
                    pe.wait_ge(S["l0_rhs"], done[c])
                    pe.wait_ge(S["l0_lhs"], done[c])
                    pe.wait_ge(S["pos_mask"], done[c])
                    t.matmul(bank_a[c][:, :], e_lhs[c][:], e_rhs[c][:].rearrange("p a k -> p (a k)"), start=True, stop=False)
                    t.matmul(bank_a[c][:, :], big_gat[:], pos_m1[c][:].rearrange("p a k -> p (a k)"),
                             start=False, stop=True).then_inc(S["l0_z"], 1)
                transposes("l0_pTp", ["l0_exp"], pr)
                attend("l0")
                transposes("l1_xTp", ["na_x", "l0_rs"], x1)
                for c in range(CHAINS):
                    pe.wait_ge(S["l1_xT"], done[c])
                    pe.wait_ge(S["l0_h"], done[c])
                    t.matmul(bank_b[c][:, :], qk[:], xT[c][:].rearrange("p a k -> p (a k)"), start=True, stop=True).then_inc(S["l1_qTp"], 1)
                for c in range(CHAINS):
                    pe.wait_ge(S["l1_qT"], done[c])
                    pe.wait_ge(S["masks"], done[c])
                    for g in range(PER_GROUP):
                        t.matmul(cut(bank_a[c], g), qT[c][:, g, :], xT[c][:, g, :], start=g == 0, stop=False, skip_group_check=True)
                    t.matmul(bank_a[c][:, :], big_att[:], zero_m[c][:].rearrange("p a k -> p (a k)"),
                             start=False, stop=True, skip_group_check=True).then_inc(S["l1_sp"], 1)
                project("l1_valp", [], bank_b, wt("WvT"))
                transposes("l1_pTp", ["l1_exp"], pr)
                attend("l1")
                transposes("n1_xTp", ["nb_x", "l1_rs"], t2)
                project("n1_hp", ["n1_xT", "l1_h"], bank_b, w1a[:], bias=0)
                transposes("n2_xTp", ["nc_x"], t1)
                project("n2_hp", ["n2_xT", "l1_leaky"], bank_b, w2a[:], bias=1)
                transposes("l2_xTp", ["ne_x"], x2)
                project("l2_hp", ["l2_xT", "nd_x"], bank_b, wt("WlT"), bias=2)
                project("l2_gp", [], bank_a, gate[:], bias=3)
                for c in range(CHAINS):
                    pe.wait_ge(S["l2_v"], done[c])
                    for g in range(PER_GROUP):
                        last = t.matmul(cut(bank_b[c], g), one_half[c][:, g, :], t2[c][:, g, :], start=True, stop=True)
                    last.then_inc(S["l2_out"], 1)
                transposes("l3_xTp", ["nf_x"], x3)
                logits("l3_ep", ["l3_xT"], slots3)
                project("l3_hp", ["l2_res"], bank_b, wt("W3T"), bias=4)
                done4 = [pe.snap(r * (CHAINS * PER_GROUP) + (c + 1)) for c in range(CHAINS * PER_GROUP)]
                for g in range(PER_GROUP):
                    for c in range(CHAINS):
                        if g == 0:
                            pe.wait_ge(S["l3_rhs"], done[c])
                            pe.wait_ge(S["l3_lhs"], done[c])
                        quad = slice(32 * g, 32 * g + 32)
                        t.matmul(bank_a[c][:, :], e_lhs[c][quad, :], e_rhs[c][quad, :, :].rearrange("p a k -> p (a k)"),
                                 start=True, stop=False)
                        t.matmul(bank_a[c][:, :].rearrange("p (h k) -> p h k", h=HEADS), big_gat[:],
                                 one_m1[c][:, g, :].unsqueeze(1).broadcast_to([P, HEADS, P]),
                                 start=False, stop=True).then_inc(S["h_z"], 1)
                    for c in range(CHAINS):
                        pe.wait_ge(S["h_exp"], done4[g * CHAINS + c])
                        for h in range(HEADS):
                            last = t.transpose(cut(bank_a[c], h), pr[c][:, h, :], ident)
                        last.then_inc(S["h_pTp"], 1)
                    for c in range(CHAINS):
                        pe.wait_ge(S["h_pT"], done4[g * CHAINS + c])
                        if g == 0:
                            pe.wait_ge(S["l3_h"], done[c])
                        else:
                            pe.wait_ge(S["h_out"], done4[(g - 1) * CHAINS + c])
                        for h in range(HEADS):
                            last = t.matmul(bank_b[c][:, h * HS:(h + 1) * HS], pT[c][:, h, :], h3[c][:, g, h, :], start=True, stop=True)
                        last.then_inc(S["h_pv"], 1)
                pe.wait_ge(S["h_out"], done4[PER_GROUP * CHAINS - 1])


def kernel(**inputs):
    import concourse.bacc as bacc
    from concourse.bass_utils import run_bass_kernel_spmd

    def f(name):
        return np.asarray(inputs[name])

    arrays = {
        "x_in": np.ascontiguousarray(f("x").transpose(1, 0, 2)),
        "adj_in": np.ascontiguousarray(f("adj").transpose(1, 0, 2)),
        "weights_in": np.ascontiguousarray(np.stack([
            f("L0_gnn_W"), f("L0_gnn_W").T, f("L1_gnn_Wq"), f("L1_gnn_Wk"), f("L1_gnn_Wv").T, f("L1_gnn_W1").T,
            f("L1_gnn_W2").T, f("L2_gnn_W_loop"), f("L2_gnn_W_loop").T, f("L2_gnn_Wg_loop").T,
            f("L3_gnn_W"), f("L3_gnn_W").T], axis=1)),
        "columns_in": np.ascontiguousarray(np.stack([
            f("L0_gnn_a")[:P, 0], f("L0_gnn_a")[P:, 0], f("L1_gnn_ln1_w"), f("L1_gnn_ln1_b"), f("L1_gnn_ln2_w"),
            f("L1_gnn_ln2_b"), f("L3_gnn_a")[:, :HEAD_C].reshape(P), f("L3_gnn_a")[:, HEAD_C:].reshape(P),
            f("L3_gnn_b")], axis=1)),
        "rows_in": np.ascontiguousarray(np.broadcast_to(np.stack([
            f("L1_gnn_b1"), f("L1_gnn_b2"), f("L2_gnn_b_loop")[0], f("L2_gnn_bg_loop")[0], f("L3_gnn_b"),
            f("L1_gnn_lnf_w"), f("L1_gnn_lnf_b")])[None], (P, len(ROWS), P))),
        "consts_in": constants(),
        "split_in": split_vectors(),
    }
    nc = bacc.Bacc("TRN2", target_bir_lowering=False, num_devices=1)
    args = [nc.dram_tensor(name, a.shape, mybir.dt.from_np(a.dtype), kind="ExternalInput").ap() for name, a in arrays.items()]
    out = nc.dram_tensor("out", (P, GRAPHS, P), F32, kind="ExternalOutput").ap()
    graph_layers_kernel(nc, *args, out)
    r = run_bass_kernel_spmd(nc, [arrays], core_ids=[0])
    return np.ascontiguousarray(r.results[0]["out"].transpose(1, 0, 2))
```

```python
from contextlib import ExitStack

import numpy as np

import concourse.bass as bass
from concourse import mybir

P = 128
GRAPHS = 64
PER_GROUP = 4
CHAINS = 4
GROUPS = GRAPHS // PER_GROUP
ROUNDS = GROUPS // CHAINS
PAIRS = CHAINS // 2
TURNS = GROUPS // 4 - 1
PITCH = 9
FIRST_PACE = 1.0
W = PER_GROUP * P
HEADS = 4
HEAD_C = P // HEADS
HS = HEAD_C + 1
ALPHA = 0.2
EPS = 1e-5
NEG_GAT = float(2.0 ** 53)
NEG_ATT = float(2.0 ** 30)

F32 = mybir.dt.float32
BF16 = mybir.dt.bfloat16
I32 = mybir.dt.int32
ALU = mybir.AluOpType
ACT = mybir.ActivationFunctionType
AX_X = mybir.AxisListType.X

WEIGHTS = ["W0", "W0T", "Wq", "Wk", "WvT", "W1T", "W2T", "Wl", "WlT", "WgT", "W3", "W3T"]
COLUMNS = ["a0_src", "a0_dst", "ln1_w", "ln1_b", "ln2_w", "ln2_b", "a3_src", "a3_dst", "b3"]
ROWS = ["b1", "b2", "b_loop", "bg_loop", "b3", "lnf_w", "lnf_b"]
VECTORS = ["s1", "s2", "src0", "dst0", "src3", "dst3", "b_s1", "b_s2", "b_keep"]
CONSTS = P + HEADS + 2 * W + len(VECTORS)
BIASES = 5


def constants():
    c = np.zeros((P, CONSTS), np.float32)
    c[:, :P] = np.eye(P)
    for h in range(HEADS):
        c[h * HEAD_C:(h + 1) * HEAD_C, P + h] = 1
    sel0 = c[:, P + HEADS:P + HEADS + W].reshape(P, PER_GROUP, P)
    sel3 = c[:, P + HEADS + W:P + HEADS + 2 * W].reshape(P, HEADS, P)
    vec = {name: c[:, P + HEADS + 2 * W + k] for k, name in enumerate(VECTORS)}
    for p in range(P):
        g, slot = divmod(p, 32)
        if slot < 24:
            sel3[p, slot % HEADS] = 1
            vec["src3" if slot < 12 else "dst3"][p] = 1
        if slot < 6:
            sel0[p, g] = 1
            vec["src0" if slot < 3 else "dst0"][p] = 1
    for p in range(3):
        vec["b_keep"][p] = 1
        vec["b_s1"][p] = -1.0 if p else 0.0
        vec["b_s2"][p] = -1.0 if p == 2 else 0.0
    return c


def split_vectors():
    s = np.zeros((P, 4), np.float32)
    for p in range(P):
        slot = p % 32
        if slot < 6:
            s[p, 0] = -1.0 if slot % 3 else 0.0
            s[p, 1] = -1.0 if slot % 3 == 2 else 0.0
        if slot < 24:
            part = (slot % 12) // HEADS
            s[p, 2] = -1.0 if part else 0.0
            s[p, 3] = -1.0 if part == 2 else 0.0
    return s


def graph_layers_kernel(nc, x_d, adj_d, w_d, col_d, row_d, const_d, split_d, out_d):
    with ExitStack() as ctx:
        def sb(name, shape, dt=F32):
            return ctx.enter_context(nc.sbuf_tensor(name, shape, dt))

        def chain_tiles(name, shape, dt=F32):
            return [sb(f"{name}{c}", shape, dt) for c in range(CHAINS)]

        def sem(name):
            return ctx.enter_context(nc.semaphore(name))

        bank_a = [ctx.enter_context(nc.psum_tensor(f"bank_a{c}", [P, W], F32)) for c in range(CHAINS)]
        bank_b = [ctx.enter_context(nc.psum_tensor(f"bank_b{c}", [P, W], F32)) for c in range(CHAINS)]

        wts = sb("wts", [P, len(WEIGHTS), P])
        cols = sb("cols", [P, len(COLUMNS)])
        rows = sb("rows", [P, len(ROWS), P])
        cst = sb("cst", [P, CONSTS])
        spl = sb("spl", [P, 4])
        qk = sb("qk", [P, P])
        w1a = sb("w1a", [P, P])
        w2a = sb("w2a", [P, P])
        gate = sb("gate", [P, P])
        a0s = sb("a0s", [P, 32])
        a3s = sb("a3s", [P, PER_GROUP, 32])
        slots0 = sb("slots0", [P, PER_GROUP, P])
        slots3 = sb("slots3", [P, PER_GROUP, P])
        kz3 = sb("kz3", [P, 1])
        ln_b_wide = sb("ln_b_wide", [P, 2, P])
        bias_f = sb("bias_f", [P, BIASES, P])
        bias_h = sb("bias_h", [P, BIASES, P], BF16)
        bias_r = sb("bias_r", [P, BIASES, P])
        bias_l = sb("bias_l", [P, BIASES, P])
        bias_parts = sb("bias_parts", [P, BIASES, P], BF16)
        ones_h = sb("ones_h", [P, P], BF16)
        ones_col = sb("ones_col", [P, 1])
        big_gat = sb("big_gat", [P, P], BF16)
        big_att = sb("big_att", [P, P], BF16)
        sel0 = sb("sel0", [P, PER_GROUP, P], BF16)
        sel3 = sb("sel3", [P, HEADS, P], BF16)
        half_pow = sb("half_pow", [P, 2 * PER_GROUP])

        def wt(name):
            return wts[:, WEIGHTS.index(name), :]

        def col(name):
            k = COLUMNS.index(name)
            return cols[:, k:k + 1]

        def row(name):
            return rows[:, ROWS.index(name), :]

        def vec(name):
            k = P + HEADS + 2 * W + VECTORS.index(name)
            return cst[:, k:k + 1]

        ident = cst[:, 0:P]
        head_of = cst[:, P:P + HEADS]

        x0 = chain_tiles("x0", [P, PER_GROUP, P])
        adj = chain_tiles("adj", [P, PER_GROUP, P], I32)
        x1 = chain_tiles("x1", [P, PER_GROUP, P])
        x2 = chain_tiles("x2", [P, PER_GROUP, P])
        x3 = chain_tiles("x3", [P, PER_GROUP, P])
        xo = chain_tiles("xo", [P, PER_GROUP, P])
        xb = chain_tiles("xb", [P, PER_GROUP, P])
        xT = chain_tiles("xT", [P, PER_GROUP, P])
        val = chain_tiles("val", [P, PER_GROUP, P])
        qT = chain_tiles("qT", [P, PER_GROUP, P])
        sc = chain_tiles("sc", [P, PER_GROUP, P])
        pr = chain_tiles("pr", [P, PER_GROUP, P])
        pT = chain_tiles("pT", [P, PER_GROUP, P])
        t1 = chain_tiles("t1", [P, PER_GROUP, P])
        t2 = chain_tiles("t2", [P, PER_GROUP, P])
        h3 = chain_tiles("h3", [P, PER_GROUP, HEADS, HS])
        pos_m1 = chain_tiles("pos_m1", [P, PER_GROUP, P], BF16)
        zero_m = chain_tiles("zero_m", [P, PER_GROUP, P], BF16)
        one_m1 = chain_tiles("one_m1", [P, PER_GROUP, P], BF16)
        one_half = chain_tiles("one_half", [P, PER_GROUP, P])
        e_f = chain_tiles("e_f", [P, P])
        e_h = chain_tiles("e_h", [P, P], BF16)
        e_r = chain_tiles("e_r", [P, P])
        e_h2 = chain_tiles("e_h2", [P, P], BF16)
        e_parts = chain_tiles("e_parts", [P, P], BF16)
        e_lhs = chain_tiles("e_lhs", [P, P], BF16)
        e_row = chain_tiles("e_row", [P, P], BF16)
        e_rhs = chain_tiles("e_rhs", [P, 4, P], BF16)
        nmax = chain_tiles("nmax", [P, PER_GROUP])
        rsum = chain_tiles("rsum", [P, PER_GROUP])
        stats = [sb(f"stats{k}", [P, 2, 2, 2, 3]) for k in range(PAIRS)]
        veps = [sb(f"veps{k}", [P, 2 * PER_GROUP]) for k in range(PAIRS)]
        rstd = [sb(f"rstd{k}", [P, 2, PER_GROUP]) for k in range(PAIRS)]

        def per_graph(tile):
            return tile[:, :].unsqueeze(2).broadcast_to([P, PER_GROUP, P])

        def mean_of(c, g):
            return stats[c // 2][:, c % 2, g // 2, g % 2, 1:2]

        def rstd_at(c, g):
            return rstd[c // 2][:, c % 2, g:g + 1]

        def bank(banks, c):
            return banks[c][:, :].rearrange("p (g k) -> p g k", g=PER_GROUP)

        def flat(tile):
            return tile[:].rearrange("p a k -> p (a k)")

        params_loaded = sem("params_loaded")
        x_loaded = [sem(f"x_loaded{c}") for c in range(CHAINS)]
        adj_loaded = [sem(f"adj_loaded{c}") for c in range(CHAINS)]
        stored = [sem(f"stored{c}") for c in range(CHAINS)]
        names = """n1_gated h_z h_relu l0_relu prep_step prep_pe prep_pow
            pos_mask masks
            l0_xTp l0_xT l0_ep l0_valp l0_val l0_ef l0_z
            l1_xTp l1_xT l1_qTp l1_qT l1_sp l1_valp l1_val l1_shift
            n1_xTp n1_xT n1_hp n1_th n2_xTp n2_xT n2_hp xb_ready n3_scaled n3_w
            l2_xTp l2_xT l2_hp l2_gp l2_th l2_v l2_out l2_res
            l3_xTp l3_xT l3_ep l3_hp l3_h l3_ef l3_out l3_res
            h_leaky h_max h_sub h_exp h_pTp h_pT h_pv h_rs h_out""".split()
        for layer in ("l0", "l3"):
            names += [f"{layer}_{s}" for s in ("eh", "er", "eh2", "parts", "lhs", "row", "rhs")]
        for layer in ("l0", "l1"):
            names += [f"{layer}_{s}" for s in ("leaky", "max", "sub", "exp", "pTp", "pT", "pv", "rs", "h", "act", "gated", "res")]
        for norm in ("na", "nb", "nc", "nd", "ne", "nf", "ng"):
            names += [f"{norm}_{s}" for s in ("stats", "veps", "rstd", "x")]
        S = {name: sem(name) for name in names}


        class Turn:

            def __init__(self, eng, q, k):
                self.eng, self.q, self.k = eng, q, k
                self.chains = (0, 1) if k % 2 == 0 else (2, 3)
                self.known = {}

            def times(self, factor, plus):
                if isinstance(self.q, int):
                    return factor * (2 * self.q + self.k) + plus
                if (factor, plus) not in self.known:
                    self.known[factor, plus] = self.eng.snap(self.q * (2 * factor) + (factor * self.k + plus))
                return self.known[factor, plus]

            def group(self, c):
                return self.times(2, c % 2 + 1)

            def pair(self):
                return self.times(1, 1)

            def head_tile(self, g, c):
                return self.times(2 * PER_GROUP, 2 * g + c % 2 + 1)

            def load(self):
                if isinstance(self.q, int):
                    return 16 * (self.q + self.k // 2 + 1)
                if "load" not in self.known:
                    self.known["load"] = self.eng.to_reg(self.q * 16 + 16 * (self.k // 2 + 1))
                return self.known["load"]

        def side_by_side(first, second):
            due = [next(first, None), next(second, None)]
            halves = (first, second)
            while due[0] is not None or due[1] is not None:
                k = 0 if due[1] is None or (due[0] is not None and due[0] * FIRST_PACE <= due[1]) else 1
                due[k] = next(halves[k], None)

        def run(eng, first, second):
            side_by_side(first(Turn(eng, 0, 0)), iter(()))
            with eng.Fori(0, TURNS) as q:
                side_by_side(first(Turn(eng, q, 1)), second(Turn(eng, q, 0)))
                side_by_side(first(Turn(eng, q, 2)), second(Turn(eng, q, 1)))
            side_by_side(first(Turn(eng, TURNS, 1)), second(Turn(eng, TURNS, 0)))
            side_by_side(iter(()), second(Turn(eng, TURNS, 1)))

        prepared = {}
        block = ctx.enter_context(nc.Block())

        @block.sync
        def _(sp):
            for dst, src in ((cst, const_d), (wts, w_d), (cols, col_d), (spl, split_d), (rows, row_d)):
                sp.dma_start(dst[:], src).then_inc(params_loaded, 16)
            for c in range(CHAINS):
                sp.dma_start(x0[c][:], x_d[:, c * PER_GROUP:(c + 1) * PER_GROUP, :]).then_inc(x_loaded[c], 16)
                sp.dma_start(adj[c][:], adj_d[:, c * PER_GROUP:(c + 1) * PER_GROUP, :]).then_inc(adj_loaded[c], 16)
            with sp.Fori(0, ROUNDS - 1) as r:
                done = [sp.to_reg(r * CHAINS + (c + 1)) for c in range(CHAINS)]
                for c in range(CHAINS):
                    sp.wait_ge(params_loaded, 16 * 5)
                    sp.wait_ge(S["l0_res"], done[c])
                    sp.wait_ge(S["masks"], done[c])
                    at = bass.ds(r * (CHAINS * PER_GROUP) + (CHAINS + c) * PER_GROUP, PER_GROUP)
                    sp.dma_start(x0[c][:], x_d[:, at, :]).then_inc(x_loaded[c], 16)
                    sp.dma_start(adj[c][:], adj_d[:, at, :]).then_inc(adj_loaded[c], 16)

        @block.vector
        def _(dve):
            steps = [0]

            def prep(ins):
                steps[0] += 1
                ins.then_inc(S["prep_step"], 1)
                dve.wait_ge(S["prep_step"], steps[0])

            v = nc.vector
            dve.wait_ge(params_loaded, 16 * 5)
            prep(v.memset(a0s[:], 0.0))
            prep(v.memset(a3s[:], 0.0))
            prep(v.memset(slots0[:], 0.0))
            prep(v.memset(slots3[:], 0.0))
            prep(v.memset(ones_h[:], 1.0))
            prep(v.memset(ones_col[:], 1.0))
            for c in range(CHAINS):
                prep(v.memset(h3[c][:, :, :, HEAD_C:HS], 1.0))
            for part in range(3):
                prep(v.tensor_copy(a0s[:, part:part + 1], col("a0_src")))
                prep(v.tensor_copy(a0s[:, 3 + part:4 + part], col("a0_dst")))
                for g in range(PER_GROUP):
                    prep(v.tensor_scalar(a3s[:, g, 4 * part:4 * part + 4], head_of, col("a3_src"), None, ALU.mult))
                    prep(v.tensor_scalar(a3s[:, g, 12 + 4 * part:16 + 4 * part], head_of, col("a3_dst"), None, ALU.mult))
            prep(v.tensor_scalar(w1a[:], wt("W1T"), col("ln1_w"), None, ALU.mult))
            prep(v.tensor_scalar(w2a[:], wt("W2T"), col("ln2_w"), None, ALU.mult))
            prep(v.tensor_copy(ln_b_wide[:, 0, :], col("ln1_b").broadcast_to([P, P])))
            prep(v.tensor_copy(ln_b_wide[:, 1, :], col("ln2_b").broadcast_to([P, P])))
            prep(v.tensor_scalar(big_gat[:], ident, NEG_GAT, None, ALU.mult))
            prep(v.tensor_scalar(big_att[:], ident, NEG_ATT, None, ALU.mult))
            prep(v.tensor_copy(sel0[:], cst[:, P + HEADS:P + HEADS + W].rearrange("p (a k) -> p a k", a=4)))
            prep(v.tensor_copy(sel3[:], cst[:, P + HEADS + W:P + HEADS + 2 * W].rearrange("p (a k) -> p a k", a=4)))
            prep(v.tensor_copy(bias_f[:, 2:5, :], rows[:, 2:5, :]))
            prepared["operands"] = steps[0]
            dve.wait_ge(S["prep_pe"], 1)
            prep(v.tensor_scalar(qk[:], bank_a[0][:, 0:P], float(P) ** -0.5, None, ALU.mult))
            prep(v.tensor_copy(gate[:], bank_a[0][:, P:2 * P]))
            for k, b in enumerate(("b1", "b2")):
                prep(v.tensor_tensor(bias_f[:, k, :], bank_a[0][:, (2 + k) * P:(3 + k) * P], row(b), ALU.add))
            for g in range(PER_GROUP):
                prep(v.tensor_copy(slots0[:, g, 32 * g:32 * g + 32], bank_b[0][:, 0:32]))
                prep(v.tensor_copy(slots3[:, g, 32 * g:32 * g + 32], bank_b[0][:, 32:64]))
            prep(v.tensor_copy(kz3[:], bank_b[0][:, 64:65]))
            prep(v.tensor_copy(bias_h[:], bias_f[:]))
            prep(v.scalar_tensor_tensor(bias_r[:], bias_h[:], vec("b_s1"), bias_f[:], ALU.mult, ALU.add))
            prep(v.tensor_copy(bias_h[:], bias_r[:]))
            prep(v.scalar_tensor_tensor(bias_l[:], bias_h[:], vec("b_s2"), bias_r[:], ALU.mult, ALU.add))
            prep(v.tensor_scalar(bias_parts[:], bias_l[:], vec("b_keep"), None, ALU.mult))
            prepared["all"] = steps[0]


            def every(u, name, after, op):
                for c in u.chains:
                    for s in after:
                        dve.wait_ge(S[s], u.group(c))
                    op(c).then_inc(S[name], 1)

            def split(u, layer, k, at, src, dst):
                yield at
                every(u, f"{layer}_eh", [f"{layer}_ef"], lambda c: v.tensor_copy(e_h[c][:], e_f[c][:]))
                yield at + 1
                every(u, f"{layer}_er", [f"{layer}_eh"], lambda c: v.scalar_tensor_tensor(
                    e_r[c][:], e_h[c][:], spl[:, k:k + 1], e_f[c][:], ALU.mult, ALU.add))
                yield at + 2
                every(u, f"{layer}_eh2", [f"{layer}_er"], lambda c: v.tensor_copy(e_h2[c][:], e_r[c][:]))
                yield at + 3
                every(u, f"{layer}_parts", [f"{layer}_eh2"], lambda c: v.scalar_tensor_tensor(
                    e_parts[c][:], e_h2[c][:], spl[:, k + 1:k + 2], e_r[c][:], ALU.mult, ALU.add))
                yield at + 4
                every(u, f"{layer}_row", [f"{layer}_parts"], lambda c: v.tensor_scalar(
                    e_row[c][:], e_parts[c][:], vec(dst), vec(src), ALU.mult, ALU.add))
                every(u, f"{layer}_lhs", [f"{layer}_parts"], lambda c: v.tensor_scalar(
                    e_lhs[c][:], e_parts[c][:], vec(src), vec(dst), ALU.mult, ALU.add))

            def layer_norm(u, norm, after, at, src, dst, eps=EPS):
                yield at
                for c in u.chains:
                    dve.wait_ge(S[after], u.group(c))
                    for k in range(2):
                        last = v.bn_stats(stats[c // 2][:, c % 2, k, :, :].rearrange("p a s -> p (a s)"),
                                          src(c)[:, 2 * k:2 * k + 2, :].rearrange("p g k -> p k g"))
                    last.then_inc(S[norm + "_stats"], 1)
                yield at + 1
                k = u.chains[0] // 2
                dve.wait_ge(S[norm + "_stats"], u.group(u.chains[1]))
                v.tensor_scalar(veps[k][:], stats[k][:, :, :, :, 2:3].rearrange("p c a b o -> p (c a b o)"),
                                1.0 / P, eps, ALU.mult, ALU.add).then_inc(S[norm + "_veps"], 1)
                yield at + 3
                for c in u.chains:
                    dve.wait_ge(S[norm + "_rstd"], u.pair())
                    for g in range(PER_GROUP):
                        last = v.tensor_scalar(dst(c)[:, g, :], src(c)[:, g, :], mean_of(c, g), rstd_at(c, g),
                                               ALU.subtract, ALU.mult)
                    last.then_inc(S[norm + "_x"], 1)

            def first(u):
                yield 0
                for c in u.chains:
                    dve.wait_ge(adj_loaded[c], u.load())
                    v.tensor_scalar(pos_m1[c][:], adj[c][:], 0.0, -1.0, ALU.is_gt, ALU.add).then_inc(S["pos_mask"], 1)
                yield 3
                for c in u.chains:
                    v.tensor_scalar(zero_m[c][:], adj[c][:], 0.0, -1.0, ALU.is_equal, ALU.mult)
                    v.tensor_scalar(one_half[c][:], adj[c][:], 1.0, 0.5, ALU.is_equal, ALU.mult)
                    v.tensor_scalar(one_m1[c][:], adj[c][:], 1.0, -1.0, ALU.is_equal, ALU.add).then_inc(S["masks"], 1)
                yield from split(u, "l0", 0, 4, "src0", "dst0")
                yield 12
                every(u, "l0_leaky", ["l0_relu"], lambda c: v.tensor_tensor(sc[c][:], bank(bank_a, c), sc[c][:], ALU.add))
                yield 13
                every(u, "l0_max", ["l0_leaky"], lambda c: v.tensor_reduce(nmax[c][:], sc[c][:], AX_X, ALU.max, negate=True))
                yield 19
                every(u, "l0_rs", ["l0_pv"], lambda c: v.reciprocal(rsum[c][:], bank_a[c][:, 0:PER_GROUP]))
                yield 22
                every(u, "l0_gated", ["l0_act"], lambda c: v.scalar_tensor_tensor(
                    t2[c][:], t2[c][:], 1.0, t1[c][:], ALU.min, ALU.max))
                yield from layer_norm(u, "na", "l0_res", 24, lambda c: t2[c], lambda c: x1[c])
                yield 32
                every(u, "l1_max", ["l1_sp"], lambda c: v.tensor_reduce(nmax[c][:], bank(bank_a, c), AX_X, ALU.max, negate=True))
                yield 37
                every(u, "l1_rs", ["l1_pv"], lambda c: v.reciprocal(rsum[c][:], bank_a[c][:, 0:PER_GROUP]))
                yield 40
                every(u, "l1_gated", ["l1_act"], lambda c: v.scalar_tensor_tensor(
                    t1[c][:], t2[c][:], 1.0, t1[c][:], ALU.add, ALU.mult))
                yield from layer_norm(u, "nb", "l1_gated", 41, lambda c: t1[c], lambda c: t2[c], 4 * EPS)
                yield 49
                every(u, "n1_gated", ["n1_th"], lambda c: v.scalar_tensor_tensor(
                    t2[c][:], t1[c][:], 1.0, bank(bank_b, c), ALU.add, ALU.mult))
                yield from layer_norm(u, "nc", "n1_gated", 50, lambda c: t2[c], lambda c: t1[c], 4 * EPS)
                yield from layer_norm(u, "nd", "n2_hp", 57, lambda c: bank(bank_b, c), lambda c: t1[c])
                yield from layer_norm(u, "ne", "l1_res", 63, lambda c: t2[c], lambda c: x2[c])

            def second(u):
                yield 4
                every(u, "l2_v", ["l2_th", "l2_hp"], lambda c: v.scalar_tensor_tensor(
                    t2[c][:], t1[c][:], 1.0, bank(bank_b, c), ALU.add, ALU.mult))
                yield 6
                every(u, "l2_res", ["l2_out"], lambda c: v.scalar_tensor_tensor(
                    t1[c][:], bank(bank_b, c), 0.0, x2[c][:], ALU.max, ALU.add))
                yield from layer_norm(u, "nf", "l2_res", 7, lambda c: t1[c], lambda c: x3[c])
                yield from split(u, "l3", 2, 14, "src3", "dst3")
                for g in range(PER_GROUP):
                    at = 22 + PITCH * g
                    yield at
                    for c in u.chains:
                        dve.wait_ge(S["h_relu"], u.head_tile(g, c))
                        v.tensor_tensor(sc[c][:], bank(bank_a, c), sc[c][:], ALU.add).then_inc(S["h_leaky"], 1)
                    yield at + 1
                    for c in u.chains:
                        dve.wait_ge(S["h_leaky"], u.head_tile(g, c))
                        v.tensor_reduce(nmax[c][:], sc[c][:], AX_X, ALU.max, negate=True).then_inc(S["h_max"], 1)
                    heads = {c: bank_b[c][:, 0:HEADS * HS].rearrange("p (h k) -> p h k", h=HEADS) for c in u.chains}
                    yield at + 7
                    for c in u.chains:
                        dve.wait_ge(S["h_pv"], u.head_tile(g, c))
                        v.reciprocal(rsum[c][:].unsqueeze(2), heads[c][:, :, HEAD_C:HS]).then_inc(S["h_rs"], 1)
                    yield at + 8
                    for c in u.chains:
                        dve.wait_ge(S["h_rs"], u.head_tile(g, c))
                        v.tensor_tensor(t1[c][:, g, :].rearrange("p (h k) -> p h k", h=HEADS), heads[c][:, :, 0:HEAD_C],
                                        rsum[c][:].unsqueeze(2).broadcast_to([P, HEADS, HEAD_C]), ALU.mult).then_inc(S["h_out"], 1)
                yield from layer_norm(u, "ng", "l3_res", 22 + PITCH * 3 + 10, lambda c: t1[c], lambda c: xo[c])

            run(dve, first, second)

        @block.gpsimd
        def _(pool):
            nc.gpsimd.memset(half_pow[:], -0.5).then_inc(S["prep_pow"], 1)
            pool.wait_ge(S["prep_pow"], 1)
            pool.wait_ge(S["prep_step"], prepared["all"])
            row_wide = [P, PER_GROUP, P]

            def add_to(u, name, after, dst, a, b, op=ALU.add):
                for c in u.chains:
                    pool.wait_ge(S[after], u.group(c))
                    nc.gpsimd.tensor_tensor(dst[c][:], a(c), b(c), op).then_inc(S[name], 1)

            def spread(u, layer, selector):
                add_to(u, f"{layer}_rhs", f"{layer}_row", e_rhs,
                       lambda c: e_row[c][:].unsqueeze(1).broadcast_to([P, 4, P]), lambda c: selector[:], ALU.mult)

            def rstd_of(u, norm):
                k = u.chains[0] // 2
                pool.wait_ge(S[norm + "_veps"], u.pair())
                nc.gpsimd.tensor_tensor(rstd[k][:].rearrange("p a g -> p (a g)"), veps[k][:], half_pow[:],
                                        ALU.pow).then_inc(S[norm + "_rstd"], 1)

            def first(u):
                yield 9
                spread(u, "l0", sel0)
                yield 14
                add_to(u, "l0_sub", "l0_max", sc, lambda c: sc[c][:], lambda c: per_graph(nmax[c]))
                yield 23
                add_to(u, "l0_res", "l0_gated", t2, lambda c: t2[c][:], lambda c: x0[c][:])
                yield 26
                rstd_of(u, "na")
                yield 30
                add_to(u, "xb_ready", "na_x", xb, lambda c: x1[c][:], lambda c: row("lnf_b").unsqueeze(1).broadcast_to(row_wide))
                yield 43
                rstd_of(u, "nb")
                yield 52
                rstd_of(u, "nc")
                yield 59
                rstd_of(u, "nd")
                yield 61
                add_to(u, "n3_w", "nd_x", t1, lambda c: t1[c][:], lambda c: row("lnf_w").unsqueeze(1).broadcast_to(row_wide), ALU.mult)
                yield 62
                add_to(u, "l1_res", "n3_w", t2, lambda c: t1[c][:], lambda c: xb[c][:])
                yield 65
                rstd_of(u, "ne")

            def second(u):
                yield 9
                rstd_of(u, "nf")
                yield 19
                spread(u, "l3", sel3)
                for g in range(PER_GROUP):
                    yield 22 + PITCH * g + 2
                    for c in u.chains:
                        pool.wait_ge(S["h_max"], u.head_tile(g, c))
                        nc.gpsimd.tensor_tensor(sc[c][:], sc[c][:], per_graph(nmax[c]), ALU.add).then_inc(S["h_sub"], 1)
                yield 22 + PITCH * 3 + 9
                for c in u.chains:
                    pool.wait_ge(S["h_out"], u.head_tile(PER_GROUP - 1, c))
                    nc.gpsimd.tensor_tensor(t1[c][:], t1[c][:], x3[c][:], ALU.add).then_inc(S["l3_res"], 1)
                yield 22 + PITCH * 3 + 12
                rstd_of(u, "ng")
                yield 22 + PITCH * 3 + 20
                for c in u.chains:
                    pool.wait_ge(stored[c], u.load())

            run(pool, first, second)

        @block.scalar
        def _(act):
            act.wait_ge(S["prep_step"], prepared["all"])

            def move(u, name, after, dst, src, func=ACT.Copy, **kw):
                for c in u.chains:
                    act.wait_ge(S[after], u.group(c))
                    nc.scalar.activation(dst(c), src(c), func, **kw).then_inc(S[name], 1)

            def a_bank(c):
                return bank(bank_a, c)

            def b_bank(c):
                return bank(bank_b, c)

            def weigh(u, layer):
                for c in u.chains:
                    act.wait_ge(S[layer + "_rs"], u.group(c))
                    for g in range(PER_GROUP):
                        last = nc.scalar.activation(t1[c][:, g, :], bank_b[c][:, g * P:(g + 1) * P], ACT.Copy,
                                                    scale=rsum[c][:, g:g + 1])
                    last.then_inc(S[layer + "_h"], 1)

            def first(u):
                yield 2
                move(u, "l0_xT", "l0_xTp", lambda c: xT[c][:], a_bank)
                yield 3
                move(u, "l0_ef", "l0_ep", lambda c: e_f[c][:], lambda c: bank_a[c][:, 0:P])
                yield 4
                move(u, "l0_val", "l0_valp", lambda c: val[c][:], b_bank, ACT.Identity, bias=1.0)
                yield 11
                move(u, "l0_relu", "l0_z", lambda c: sc[c][:], a_bank, ACT.Relu, scale=1 / ALPHA - 1)
                yield 15
                move(u, "l0_exp", "l0_sub", lambda c: pr[c][:], lambda c: sc[c][:], ACT.Exp, scale=ALPHA)
                yield 17
                move(u, "l0_pT", "l0_pTp", lambda c: pT[c][:], a_bank)
                yield 20
                weigh(u, "l0")
                yield 21
                move(u, "l0_act", "l0_h", lambda c: t2[c][:], lambda c: t1[c][:], ACT.Exp, bias=-1.0)
                yield 29
                move(u, "l1_xT", "l1_xTp", lambda c: xT[c][:], a_bank)
                yield 30
                move(u, "l1_qT", "l1_qTp", lambda c: qT[c][:], b_bank)
                yield 32
                move(u, "l1_val", "l1_valp", lambda c: val[c][:], b_bank)
                yield 33
                for c in u.chains:
                    act.wait_ge(S["l1_max"], u.group(c))
                    for g in range(PER_GROUP):
                        last = nc.scalar.activation(pr[c][:, g, :], bank_a[c][:, g * P:(g + 1) * P], ACT.Exp,
                                                    bias=nmax[c][:, g:g + 1])
                    last.then_inc(S["l1_exp"], 1)
                yield 35
                move(u, "l1_pT", "l1_pTp", lambda c: pT[c][:], a_bank)
                yield 38
                weigh(u, "l1")
                yield 39
                move(u, "l1_act", "l1_h", lambda c: t2[c][:], lambda c: t1[c][:], ACT.Tanh, scale=0.5)
                yield 46
                move(u, "n1_xT", "n1_xTp", lambda c: xT[c][:], a_bank)
                yield 48
                move(u, "n1_th", "n1_hp", lambda c: t1[c][:], b_bank, ACT.Tanh, scale=0.5)
                yield 55
                move(u, "n2_xT", "n2_xTp", lambda c: xT[c][:], a_bank)

            def second(u):
                yield 1
                move(u, "l2_xT", "l2_xTp", lambda c: xT[c][:], a_bank)
                yield 3
                move(u, "l2_th", "l2_gp", lambda c: t1[c][:], a_bank, ACT.Tanh, scale=0.5)
                yield 12
                move(u, "l3_xT", "l3_xTp", lambda c: xT[c][:], a_bank)
                yield 14
                move(u, "l3_ef", "l3_ep", lambda c: e_f[c][:], lambda c: bank_a[c][:, 0:P], ACT.Identity, bias=kz3[:, 0:1])
                yield 15
                move(u, "l3_h", "l3_hp", lambda c: h3[c][:, :, :, 0:HEAD_C],
                     lambda c: bank_b[c][:, :].rearrange("p (g h k) -> p g h k", g=PER_GROUP, h=HEADS))
                for g in range(PER_GROUP):
                    at = 22 + PITCH * g
                    yield at - 1
                    for c in u.chains:
                        act.wait_ge(S["h_z"], u.head_tile(g, c))
                        nc.scalar.activation(sc[c][:], a_bank(c), ACT.Relu, scale=1 / ALPHA - 1).then_inc(S["h_relu"], 1)
                    yield at + 3
                    for c in u.chains:
                        act.wait_ge(S["h_sub"], u.head_tile(g, c))
                        nc.scalar.activation(pr[c][:], sc[c][:], ACT.Exp, scale=ALPHA).then_inc(S["h_exp"], 1)
                    yield at + 5
                    for c in u.chains:
                        act.wait_ge(S["h_pTp"], u.head_tile(g, c))
                        nc.scalar.activation(pT[c][:], a_bank(c), ACT.Copy).then_inc(S["h_pT"], 1)
                yield 22 + PITCH * 3 + 14
                for c in u.chains:
                    act.wait_ge(S["ng_x"], u.group(c))
                    if isinstance(u.q, int):
                        at = slice((2 * (2 * u.q + u.k) + c % 2) * PER_GROUP, (2 * (2 * u.q + u.k) + c % 2 + 1) * PER_GROUP)
                    else:
                        at = bass.ds(u.q * (4 * PER_GROUP) + (2 * u.k + c % 2) * PER_GROUP, PER_GROUP)
                    act.dma_start(out_d[:, at, :], xo[c][:]).then_inc(stored[c], 16)

            run(act, first, second)

        @block.tensor
        def _(pe):
            t = nc.tensor
            pe.wait_ge(params_loaded, 16 * 5)
            pe.wait_ge(S["prep_step"], prepared["operands"])
            t.matmul(bank_a[0][:, 0:P], wt("Wq"), wt("Wk"), start=True, stop=True)
            t.matmul(bank_a[0][:, P:2 * P], wt("Wl"), wt("WgT"), start=True, stop=True)
            t.matmul(bank_a[0][:, 2 * P:3 * P], ln_b_wide[:, 0, :], wt("W1T"), start=True, stop=True)
            t.matmul(bank_a[0][:, 3 * P:4 * P], ln_b_wide[:, 1, :], wt("W2T"), start=True, stop=True)
            t.matmul(bank_b[0][:, 0:32], wt("W0T"), a0s[:], start=True, stop=True)
            t.matmul(bank_b[0][:, 32:64], wt("W3"), a3s[:, 0, :], start=True, stop=True)
            t.matmul(bank_b[0][:, 64:65], a3s[:].rearrange("p g s -> p (g s)"), col("b3"),
                     start=True, stop=True).then_inc(S["prep_pe"], 1)
            pe.wait_ge(S["prep_step"], prepared["all"])

            def cut(banks, c, g):
                return banks[c][:, g * P:(g + 1) * P]

            def transposes(u, name, after, src):
                for c in u.chains:
                    for s in after:
                        pe.wait_ge(S[s], u.group(c))
                    for g in range(PER_GROUP):
                        last = t.transpose(cut(bank_a, c, g), src[c][:, g, :], ident)
                    last.then_inc(S[name], 1)

            def project(u, name, after, banks, weights, bias=None):
                for c in u.chains:
                    for s in after:
                        pe.wait_ge(S[s], u.group(c))
                    if bias is not None:
                        t.matmul(bank(banks, c), ones_h[:], bias_parts[:, bias, :].unsqueeze(1).broadcast_to([P, PER_GROUP, P]),
                                 start=True, stop=False, skip_group_check=True)
                    for g in range(PER_GROUP):
                        last = t.matmul(cut(banks, c, g), xT[c][:, g, :], weights, start=bias is None and g == 0,
                                        stop=g == PER_GROUP - 1, skip_group_check=True)
                    last.then_inc(S[name], 1)

            def logits(u, name, after, slots):
                for c in u.chains:
                    for s in after:
                        pe.wait_ge(S[s], u.group(c))
                    for g in range(PER_GROUP):
                        last = t.matmul(bank_a[c][:, 0:P], slots[:, g, :], xT[c][:, g, :], start=g == 0, stop=g == PER_GROUP - 1)
                    last.then_inc(S[name], 1)

            def attend(u, layer):
                for c in u.chains:
                    pe.wait_ge(S[layer + "_pT"], u.group(c))
                    pe.wait_ge(S[layer + "_val"], u.group(c))
                    for g in range(PER_GROUP):
                        t.matmul(cut(bank_b, c, g), pT[c][:, g, :], val[c][:, g, :], start=True, stop=True)
                    for g in range(PER_GROUP):
                        last = t.matmul(bank_a[c][:, g:g + 1], pT[c][:, g, :], ones_col[:], start=True, stop=True)
                    last.then_inc(S[layer + "_pv"], 1)

            def first(u):
                yield 1
                for c in u.chains:
                    pe.wait_ge(x_loaded[c], u.load())
                    for g in range(PER_GROUP):
                        last = t.transpose(cut(bank_a, c, g), x0[c][:, g, :], ident)
                    last.then_inc(S["l0_xTp"], 1)
                yield 2
                logits(u, "l0_ep", ["l0_xT"], slots0)
                yield 3
                project(u, "l0_valp", [], bank_b, wt("W0"))
                yield 10
                for c in u.chains:
                    for s in ("l0_rhs", "l0_lhs", "pos_mask"):
                        pe.wait_ge(S[s], u.group(c))
                    t.matmul(bank_a[c][:, :], e_lhs[c][:], flat(e_rhs[c]), start=True, stop=False)
                    t.matmul(bank_a[c][:, :], big_gat[:], flat(pos_m1[c]), start=False, stop=True).then_inc(S["l0_z"], 1)
                yield 16
                transposes(u, "l0_pTp", ["l0_exp"], pr)
                yield 18
                attend(u, "l0")
                yield 28
                transposes(u, "l1_xTp", ["na_x", "l0_rs"], x1)
                yield 29
                for c in u.chains:
                    pe.wait_ge(S["l1_xT"], u.group(c))
                    pe.wait_ge(S["l0_h"], u.group(c))
                    t.matmul(bank_b[c][:, :], qk[:], flat(xT[c]), start=True, stop=True).then_inc(S["l1_qTp"], 1)
                yield 31
                for c in u.chains:
                    pe.wait_ge(S["l1_qT"], u.group(c))
                    pe.wait_ge(S["masks"], u.group(c))
                    for g in range(PER_GROUP):
                        t.matmul(cut(bank_a, c, g), qT[c][:, g, :], xT[c][:, g, :], start=g == 0, stop=False, skip_group_check=True)
                    t.matmul(bank_a[c][:, :], big_att[:], flat(zero_m[c]),
                             start=False, stop=True, skip_group_check=True).then_inc(S["l1_sp"], 1)
                project(u, "l1_valp", [], bank_b, wt("WvT"))
                yield 34
                transposes(u, "l1_pTp", ["l1_exp"], pr)
                yield 36
                attend(u, "l1")
                yield 45
                transposes(u, "n1_xTp", ["nb_x", "l1_rs"], t2)
                yield 47
                project(u, "n1_hp", ["n1_xT", "l1_h"], bank_b, w1a[:], bias=0)
                yield 54
                transposes(u, "n2_xTp", ["nc_x"], t1)
                yield 56
                project(u, "n2_hp", ["n2_xT", "n1_gated"], bank_b, w2a[:], bias=1)

            def second(u):
                yield 0
                transposes(u, "l2_xTp", ["ne_x"], x2)
                yield 2
                project(u, "l2_gp", ["l2_xT"], bank_a, gate[:], bias=3)
                project(u, "l2_hp", ["nd_x"], bank_b, wt("WlT"), bias=2)
                yield 5
                for c in u.chains:
                    pe.wait_ge(S["l2_v"], u.group(c))
                    for g in range(PER_GROUP):
                        last = t.matmul(cut(bank_b, c, g), one_half[c][:, g, :], t2[c][:, g, :], start=True, stop=True)
                    last.then_inc(S["l2_out"], 1)
                yield 11
                transposes(u, "l3_xTp", ["nf_x"], x3)
                yield 13
                logits(u, "l3_ep", ["l3_xT"], slots3)
                project(u, "l3_hp", ["l2_res"], bank_b, wt("W3T"), bias=4)
                for g in range(PER_GROUP):
                    at = 22 + PITCH * g
                    yield at - 2
                    for c in u.chains:
                        if g == 0:
                            pe.wait_ge(S["l3_rhs"], u.group(c))
                            pe.wait_ge(S["l3_lhs"], u.group(c))
                        quad = slice(32 * g, 32 * g + 32)
                        t.matmul(bank_a[c][:, :], e_lhs[c][quad, :], e_rhs[c][quad, :, :].rearrange("p a k -> p (a k)"),
                                 start=True, stop=False)
                        t.matmul(bank(bank_a, c), big_gat[:], one_m1[c][:, g, :].unsqueeze(1).broadcast_to([P, HEADS, P]),
                                 start=False, stop=True).then_inc(S["h_z"], 1)
                    yield at + 4
                    for c in u.chains:
                        pe.wait_ge(S["h_exp"], u.head_tile(g, c))
                        for h in range(HEADS):
                            last = t.transpose(cut(bank_a, c, h), pr[c][:, h, :], ident)
                        last.then_inc(S["h_pTp"], 1)
                    yield at + 6
                    for c in u.chains:
                        pe.wait_ge(S["h_pT"], u.head_tile(g, c))
                        if g == 0:
                            pe.wait_ge(S["l3_h"], u.group(c))
                        else:
                            pe.wait_ge(S["h_out"], u.head_tile(g - 1, c))
                        for h in range(HEADS):
                            last = t.matmul(bank_b[c][:, h * HS:(h + 1) * HS], pT[c][:, h, :], h3[c][:, g, h, :], start=True, stop=True)
                        last.then_inc(S["h_pv"], 1)
                yield 22 + PITCH * 3 + 9
                pe.wait_ge(S["h_out"], u.head_tile(PER_GROUP - 1, u.chains[1]))

            run(pe, first, second)


def kernel(**inputs):
    import concourse.bacc as bacc
    from concourse.bass_utils import run_bass_kernel_spmd

    def f(name):
        return np.asarray(inputs[name])

    arrays = {
        "x_in": np.ascontiguousarray(f("x").transpose(1, 0, 2)),
        "adj_in": np.ascontiguousarray(f("adj").transpose(1, 0, 2)),
        "weights_in": np.ascontiguousarray(np.stack([
            f("L0_gnn_W"), f("L0_gnn_W").T, f("L1_gnn_Wq"), f("L1_gnn_Wk"), f("L1_gnn_Wv").T, f("L1_gnn_W1").T,
            f("L1_gnn_W2").T, f("L2_gnn_W_loop"), f("L2_gnn_W_loop").T, f("L2_gnn_Wg_loop").T,
            f("L3_gnn_W"), f("L3_gnn_W").T], axis=1)),
        "columns_in": np.ascontiguousarray(np.stack([
            f("L0_gnn_a")[:P, 0], f("L0_gnn_a")[P:, 0], f("L1_gnn_ln1_w"), f("L1_gnn_ln1_b"), f("L1_gnn_ln2_w"),
            f("L1_gnn_ln2_b"), f("L3_gnn_a")[:, :HEAD_C].reshape(P), f("L3_gnn_a")[:, HEAD_C:].reshape(P),
            f("L3_gnn_b")], axis=1)),
        "rows_in": np.ascontiguousarray(np.broadcast_to(np.stack([
            f("L1_gnn_b1"), f("L1_gnn_b2"), f("L2_gnn_b_loop")[0], f("L2_gnn_bg_loop")[0], f("L3_gnn_b"),
            f("L1_gnn_lnf_w"), f("L1_gnn_lnf_b")])[None], (P, len(ROWS), P))),
        "consts_in": constants(),
        "split_in": split_vectors(),
    }
    nc = bacc.Bacc("TRN2", target_bir_lowering=False, num_devices=1)
    args = [nc.dram_tensor(name, a.shape, mybir.dt.from_np(a.dtype), kind="ExternalInput").ap() for name, a in arrays.items()]
    out = nc.dram_tensor("out", (P, GRAPHS, P), F32, kind="ExternalOutput").ap()
    graph_layers_kernel(nc, *args, out)
    r = run_bass_kernel_spmd(nc, [arrays], core_ids=[0])
    return np.ascontiguousarray(r.results[0]["out"].transpose(1, 0, 2))
```

```python
from contextlib import ExitStack

import numpy as np

import concourse.bass as bass
from concourse import mybir

P = 128
GRAPHS = 64
PER_GROUP = 4
CHAINS = 4
GROUPS = GRAPHS // PER_GROUP
ROUNDS = GROUPS // CHAINS
INTERVAL = 32.81
ROUND = CHAINS * INTERVAL
FLAG_READ = 48
BIASES_DUE = 2
W = PER_GROUP * P
HEADS = 4
HEAD_C = P // HEADS
HS = HEAD_C + 1
ALPHA = 0.2
EPS = 1e-5
NEG_GAT = float(2.0 ** 53)
NEG_ATT = float(2.0 ** 30)

F32 = mybir.dt.float32
BF16 = mybir.dt.bfloat16
I32 = mybir.dt.int32
ALU = mybir.AluOpType
ACT = mybir.ActivationFunctionType
AX_X = mybir.AxisListType.X

WEIGHTS = ["W0", "W0T", "Wq", "Wk", "WvT", "W1T", "W2T", "Wl", "WlT", "WgT", "W3", "W3T"]
COLUMNS = ["a0_src", "a0_dst", "ln1_w", "ln1_b", "ln2_w", "ln2_b", "a3_src", "a3_dst", "b3"]
ROWS = ["b1", "b2", "b_loop", "bg_loop", "b3", "lnf_w", "lnf_b"]
VECTORS = ["s1", "s2", "src0", "dst0", "src3", "dst3", "b_s1", "b_s2", "b_keep"]
CONSTS = P + HEADS + 2 * W + len(VECTORS)
BIASES = 5
NORMS = ("na", "nb", "nc", "nd", "ne", "nf", "ng")
ACT_NORMS = ("na", "ne")
POOL_NORMS = ("nb", "nc", "nf", "ng")
SHARED_NORMS = tuple(n for n in NORMS if n in ACT_NORMS + POOL_NORMS)
FIRST_REL = 2
RELS = 39
SCAN = PER_GROUP
SCANS = GRAPHS // SCAN

DUE = {
    "pos_mask": 1.11, "masks": 1.55, "l0_xTp": 0.73, "l0_xT": 0.77, "l0_ep": 1.65, "l0_valp": 6.94, "l0_ef": 2.69,
    "l0_val": 8.68, "l0_eh": 3.13, "l0_er": 4.41, "l0_eh2": 5.21, "l0_parts": 5.43, "l0_row": 6.02, "l0_rhs": 6.86,
    "l0_lhs": 7.23, "one_mask": 12.84, "l0_z": 8.46, "l0_relu": 9.3, "l0_leaky": 9.44, "l0_max": 11.82,
    "l0_exp": 13.23, "l0_rs": 14.94, "l0_pTp": 13.78, "l0_pT": 14.93, "l0_pv": 16.62, "l0_h": 17.48, "l0_act": 18.47,
    "l0_gated": 19.1, "l0_res": 19.44, "na_stats": 21.21, "na_veps": 22.0, "na_rstd": 22.81, "na_off": 24.61,
    "na_x": 24.68, "na_y": 25.47, "xb_ready": 36.65, "l1_xTp": 25.97, "l1_xT": 26.42, "l1_qTp": 26.82, "l1_qT": 28.71,
    "l1_sp": 29.2, "l1_valp": 29.82, "l1_val": 32.42, "l1_max": 31.09, "l1_exp": 32.72, "l1_rs": 34.43,
    "l1_pTp": 34.12, "l1_pT": 35.28, "l1_pv": 36.19, "l1_h": 36.76, "l1_act": 37.13, "l1_gated": 38.38,
    "nb_stats": 39.09, "nb_veps": 39.44, "nb_rstd": 40.27, "nb_centred": 40.89, "nb_x": 41.54, "nb_y": 41.64,
    "n1_xTp": 42.03, "n1_xT": 44.24, "n1_hp": 46.28, "n1_th": 47.12, "n1_gated": 47.2, "nc_stats": 47.86,
    "nc_veps": 48.0, "nc_rstd": 48.33, "nc_centred": 49.29, "nc_x": 50.64, "nc_y": 49.34, "n2_xTp": 53.88,
    "n2_xT": 53.93, "n2_hp": 55.84, "nd_stats": 57.76, "nd_veps": 58.63, "nd_rstd": 58.97, "nd_x": 61.48,
    "n3_w": 65.42, "l1_res": 65.66, "ne_stats": 66.62, "ne_veps": 67.09, "ne_rstd": 67.15, "ne_off": 68.08,
    "ne_x": 68.42, "ne_y": 70.81, "l2_xTp": 72.7, "l2_xT": 74.18, "l2_gp": 74.2, "l2_hp": 77.04, "l2_th": 76.79,
    "l2_v": 78.42, "relations": 79.85, "l2_out": 80.22, "l2_res": 81.62, "nf_stats": 81.89, "nf_veps": 86.37,
    "nf_rstd": 86.43, "nf_centred": 90.14, "nf_x": 90.03, "nf_y": 90.38, "l3_xTp": 92.1, "l3_xT": 93.46,
    "l3_ep": 94.34, "l3_hp": 98.84, "l3_ef": 94.47, "l3_h": 102.2, "l3_eh": 94.64, "l3_er": 95.13, "l3_eh2": 95.29,
    "l3_parts": 97.21, "l3_row": 97.53, "l3_rhs": 98.0, "l3_lhs": 98.82, "h_z": (99.5, 105.38, 116.51, 122.72),
    "h_relu": (100.31, 108.52, 118.02, 124.06), "h_leaky": (100.72, 110.57, 118.93, 124.79),
    "h_max": (101.83, 110.63, 119.23, 125.13), "h_exp": (103.95, 114.33, 121.09, 128.67),
    "h_pTp": (106.4, 118.9, 122.28, 132.13), "h_pT": (107.51, 119.27, 122.43, 133.93),
    "h_pv": (112.14, 119.57, 122.89, 135.09), "h_rs": (113.57, 121.27, 126.18, 135.75),
    "h_out": (114.46, 121.49, 127.4, 136.56), "l3_res": 137.93, "ng_stats": 139.55, "ng_veps": 139.63,
    "ng_rstd": 143.3, "ng_centred": 143.54, "ng_x": 144.83, "ng_y": 144.59, "store": 146.12,
    "released": (130.31, 137.76), "stored": 171.12, "__B": 2,
}


def constants():
    c = np.zeros((P, CONSTS), np.float32)
    c[:, :P] = np.eye(P)
    for h in range(HEADS):
        c[h * HEAD_C:(h + 1) * HEAD_C, P + h] = 1
    sel0 = c[:, P + HEADS:P + HEADS + W].reshape(P, PER_GROUP, P)
    sel3 = c[:, P + HEADS + W:P + HEADS + 2 * W].reshape(P, HEADS, P)
    vec = {name: c[:, P + HEADS + 2 * W + k] for k, name in enumerate(VECTORS)}
    for p in range(P):
        g, slot = divmod(p, 32)
        if slot < 24:
            sel3[p, slot % HEADS] = 1
            vec["src3" if slot < 12 else "dst3"][p] = 1
        if slot < 6:
            sel0[p, g] = 1
            vec["src0" if slot < 3 else "dst0"][p] = 1
    for p in range(3):
        vec["b_keep"][p] = 1
        vec["b_s1"][p] = -1.0 if p else 0.0
        vec["b_s2"][p] = -1.0 if p == 2 else 0.0
    return c


def split_vectors():
    s = np.zeros((P, 4), np.float32)
    for p in range(P):
        slot = p % 32
        if slot < 6:
            s[p, 0] = -1.0 if slot % 3 else 0.0
            s[p, 1] = -1.0 if slot % 3 == 2 else 0.0
        if slot < 24:
            part = (slot % 12) // HEADS
            s[p, 2] = -1.0 if part else 0.0
            s[p, 3] = -1.0 if part == 2 else 0.0
    return s


def graph_layers_kernel(nc, x_d, adj_d, w_d, col_d, row_d, const_d, split_d, rel_w_d, rel_b_d, out_d):
    with ExitStack() as ctx:
        def sb(name, shape, dt=F32):
            return ctx.enter_context(nc.sbuf_tensor(name, shape, dt))

        def chain_tiles(name, shape, dt=F32):
            return [sb(f"{name}{c}", shape, dt) for c in range(CHAINS)]

        def sem(name):
            return ctx.enter_context(nc.semaphore(name))

        bank_a = [ctx.enter_context(nc.psum_tensor(f"bank_a{c}", [P, W], F32)) for c in range(CHAINS)]
        bank_b = [ctx.enter_context(nc.psum_tensor(f"bank_b{c}", [P, W], F32)) for c in range(CHAINS)]

        wts = sb("wts", [P, len(WEIGHTS), P])
        cols = sb("cols", [P, len(COLUMNS)])
        rows = sb("rows", [P, len(ROWS), P])
        cst = sb("cst", [P, CONSTS])
        spl = sb("spl", [P, 4])
        qk = sb("qk", [P, P])
        w1a = sb("w1a", [P, P])
        w2a = sb("w2a", [P, P])
        gate = sb("gate", [P, P])
        wl_half = sb("wl_half", [P, P])
        a0s = sb("a0s", [P, 32])
        a3s = sb("a3s", [P, PER_GROUP, 32])
        slots0 = sb("slots0", [P, PER_GROUP, P])
        slots3 = sb("slots3", [P, PER_GROUP, P])
        kz3 = sb("kz3", [P, 1])
        ln_b_wide = sb("ln_b_wide", [P, 2, P])
        bias_f = sb("bias_f", [P, BIASES, P])
        bias_h = sb("bias_h", [P, BIASES, P], BF16)
        bias_r = sb("bias_r", [P, BIASES, P])
        bias_l = sb("bias_l", [P, BIASES, P])
        bias_parts = sb("bias_parts", [P, BIASES, P], BF16)
        ones_h = sb("ones_h", [P, P], BF16)
        big_gat = sb("big_gat", [P, P], BF16)
        big_att = sb("big_att", [P, P], BF16)
        sel0 = sb("sel0", [P, PER_GROUP, P], BF16)
        sel3 = sb("sel3", [P, HEADS, P], BF16)
        rel_w = sb("rel_w", [P, 4, P])
        rel_b = sb("rel_b", [P, 4, P])
        scan = [sb(f"scan{k}", [P, SCAN, P], I32) for k in range(2)]
        rel_id = sb("rel_id", [P, 1])
        scan_max = sb("scan_max", [P, SCANS])
        any_max = sb("any_max", [P, 1])
        top = sb("top", [1, 1])
        flag = sb("flag", [1, 1], I32)
        minus_one = sb("minus_one", [P, 1])
        warm = sb("warm", [P, PER_GROUP])
        half_pow = sb("half_pow", [P, PER_GROUP])

        def wt(name):
            return wts[:, WEIGHTS.index(name), :]

        def col(name):
            k = COLUMNS.index(name)
            return cols[:, k:k + 1]

        def row(name):
            return rows[:, ROWS.index(name), :]

        def vec(name):
            k = P + HEADS + 2 * W + VECTORS.index(name)
            return cst[:, k:k + 1]

        ident = cst[:, 0:P]
        head_of = cst[:, P:P + HEADS]

        x0 = chain_tiles("x0", [P, PER_GROUP, P])
        adj = chain_tiles("adj", [P, PER_GROUP, P], I32)
        x1 = chain_tiles("x1", [P, PER_GROUP, P])
        x2 = chain_tiles("x2", [P, PER_GROUP, P])
        x3 = chain_tiles("x3", [P, PER_GROUP, P])
        xo = chain_tiles("xo", [P, PER_GROUP, P])
        xb = chain_tiles("xb", [P, PER_GROUP, P])
        xT = chain_tiles("xT", [P, PER_GROUP, P])
        val = chain_tiles("val", [P, PER_GROUP, P])
        qT = chain_tiles("qT", [P, PER_GROUP, P])
        sc = chain_tiles("sc", [P, PER_GROUP, P])
        pr = chain_tiles("pr", [P, PER_GROUP, P])
        pT = chain_tiles("pT", [P, PER_GROUP, P])
        t1 = chain_tiles("t1", [P, PER_GROUP, P])
        t2 = chain_tiles("t2", [P, PER_GROUP, P])
        h3 = chain_tiles("h3", [P, PER_GROUP, HEADS, HS])
        pos_m1 = chain_tiles("pos_m1", [P, PER_GROUP, P], BF16)
        zero_m = chain_tiles("zero_m", [P, PER_GROUP, P], BF16)
        one_m1 = chain_tiles("one_m1", [P, PER_GROUP, P], BF16)
        one_m = chain_tiles("one_m", [P, PER_GROUP, P])
        e_f = chain_tiles("e_f", [P, P])
        e_h = chain_tiles("e_h", [P, P], BF16)
        e_r = chain_tiles("e_r", [P, P])
        e_h2 = chain_tiles("e_h2", [P, P], BF16)
        e_parts = chain_tiles("e_parts", [P, P], BF16)
        e_lhs = chain_tiles("e_lhs", [P, P], BF16)
        e_row = chain_tiles("e_row", [P, P], BF16)
        e_rhs = chain_tiles("e_rhs", [P, 4, P], BF16)
        nmax = chain_tiles("nmax", [P, PER_GROUP])
        rsum = chain_tiles("rsum", [P, PER_GROUP])
        rowsum = chain_tiles("rowsum", [P, PER_GROUP])
        stats = chain_tiles("stats", [P, 2, 2, 3])
        veps = chain_tiles("veps", [P, PER_GROUP])
        rstd = chain_tiles("rstd", [P, PER_GROUP])
        offset = chain_tiles("offset", [P, PER_GROUP // 2])

        h_sc, h_pr, h_pT = ([(sc[c], val[c]) for c in range(CHAINS)], [(pr[c], qT[c]) for c in range(CHAINS)],
                            [(pT[c], xb[c]) for c in range(CHAINS)])
        h_nmax = chain_tiles("h_nmax", [P, 2, HEADS])
        h_rsum = chain_tiles("h_rsum", [P, 2, HEADS])

        def head_bank(u, g):
            return (bank_b if g % 2 else bank_a)[u.c][:, :]

        def mean_of(c, g):
            return stats[c][:, g // 2, g % 2, 1:2]

        def rstd_at(c, g):
            return rstd[c][:, g:g + 1]

        def bank(banks, c):
            return banks[c][:, :].rearrange("p (g k) -> p g k", g=PER_GROUP)

        def flat(tile):
            return tile[:].rearrange("p a k -> p (a k)")

        params_loaded = sem("params_loaded")
        rel_w_loaded = sem("rel_w_loaded")
        scan_loaded = [sem(f"scan_loaded{k}") for k in range(2)]
        rel_adj_loaded = sem("rel_adj_loaded")
        rel_b_loaded = sem("rel_b_loaded")
        x_loaded = [sem(f"x_loaded{c}") for c in range(CHAINS)]
        adj_loaded = [sem(f"adj_loaded{c}") for c in range(CHAINS)]
        stored = [sem(f"stored{c}") for c in range(CHAINS)]
        names = """n1_gated h_z h_relu l0_relu l0_leaky prep_step prep_pe prep_pow prep_act
            pos_mask masks one_mask
            l0_xTp l0_xT l0_ep l0_valp l0_val l0_ef l0_z
            l1_xTp l1_xT l1_qTp l1_qT l1_sp l1_valp l1_val
            n1_xTp n1_xT n1_hp n1_th n2_xTp n2_xT n2_hp xb_ready n3_w
            l2_xTp l2_xT l2_hp l2_gp l2_th l2_v l2_out l2_res
            l3_xTp l3_xT l3_ep l3_hp l3_h l3_ef l3_res
            h_leaky h_max h_exp h_pTp h_pT h_pv h_rs h_out""".split()
        names += """scan_step scan_row flag_set
            rel_adjTp rel_adjT rel_hTp rel_hT rel_gp rel_g rel_zero
            rel_id_set rel_u rel_th rel_a rel_v rel_mm rel_out rel_extra rel_added""".split()
        for layer in ("l0", "l3"):
            names += [f"{layer}_{s}" for s in ("eh", "er", "eh2", "parts", "lhs", "row", "rhs")]
        for layer in ("l0", "l1"):
            names += [f"{layer}_{s}" for s in ("max", "exp", "pTp", "pT", "pv", "rs", "h", "act", "gated", "res")]
        S = {name: sem(name) for name in names}
        norm_steps = {s: [sem(f"norm_{s}{c}") for c in range(CHAINS)] for s in ("stats", "veps", "rstd", "off", "centred", "x", "y")}


        class Group:

            def __init__(self, eng, q, later, c, known):
                self.eng, self.q, self.later, self.c, self.known = eng, q, later, c, known

            def times(self, factor, plus):
                plus += factor * (CHAINS * self.later + self.c)
                if isinstance(self.q, int):
                    return factor * CHAINS * self.q + plus
                if (factor, plus) not in self.known:
                    self.known[factor, plus] = self.eng.snap(self.q * (factor * CHAINS) + plus)
                return self.known[factor, plus]

            def done(self):
                return self.times(1, 1)

            def sem(self, step):
                return norm_steps[step[3:]][self.c] if step[:2] in NORMS else S[step]

            def normed(self, norm):
                return [norm + "_x"] + [norm + "_y"] * (norm in SHARED_NORMS)

            def count(self, step):
                if step[:2] not in NORMS:
                    return self.done()
                norms = {"off": ACT_NORMS, "centred": POOL_NORMS, "y": SHARED_NORMS}.get(step[3:], NORMS)
                plus = len(norms) * self.later + norms.index(step[:2]) + 1
                if isinstance(self.q, int):
                    return len(norms) * self.q + plus
                if (norms, plus) not in self.known:
                    self.known[norms, plus] = self.eng.snap(self.q * len(norms) + plus)
                return self.known[norms, plus]

            def graph_done(self, g):
                return self.times(PER_GROUP, g + 1)

            def nth(self, per_group, k, step=None):
                at = self.times(per_group, k + 1)
                return at if step is None else self.eng.to_reg(step + at)

            def loads(self, per_group, step):
                return self.eng.to_reg(step * 16 + self.times(16 * per_group, 16))

            def chain_load(self):
                if isinstance(self.q, int):
                    return 16 * (self.q + self.later + 1)
                if ("load", self.later) not in self.known:
                    self.known["load", self.later] = self.eng.to_reg(self.q * 16 + 16 * (self.later + 1))
                return self.known["load", self.later]

            def graphs(self):
                at = PER_GROUP * (CHAINS * self.later + self.c)
                if isinstance(self.q, int):
                    at += self.q * CHAINS * PER_GROUP
                    return slice(at, at + PER_GROUP)
                return bass.ds(self.q * (CHAINS * PER_GROUP) + at, PER_GROUP)

        def due(step):
            if isinstance(step, tuple):
                return DUE[step[0]][step[1]]
            return DUE[step] if isinstance(step, str) else step

        def interleave(programs):
            at = {}

            def go_on(k, here):
                program, start, first, end = programs[k]
                at.pop(k, None)
                try:
                    time = due(program.send(here))
                    while not first <= time < end:
                        time = due(program.send(False))
                    at[k] = start + time
                except StopIteration:
                    pass

            for k in range(len(programs)):
                go_on(k, None)
            while at:
                go_on(min(at, key=lambda k: (at[k], k)), True)

        def a_round(eng, group, heads, q, starts=True, ends=True, look=None):
            known = {}
            later = 0 if isinstance(q, int) else 1
            programs = [(look, 0, 0, ROUND)] if look else []
            for c in range(CHAINS):
                over = ROUND - c * INTERVAL
                for there, back, start, first, end in ((ends, 1, -over, over, 2 * ROUND), (starts, 0, c * INTERVAL, 0, over)):
                    if there:
                        u = Group(eng, q, later - back, c, known)
                        programs.append((group(u), start, first, end))
                        programs += [(heads(u, g), start, first, end) for g in range(PER_GROUP) if heads]
            interleave(programs)

        def run(eng, group, heads, look=None):
            a_round(eng, group, heads, 0, ends=False, look=look)
            with eng.Fori(0, ROUNDS - 1) as q:
                a_round(eng, group, heads, q)
            a_round(eng, group, heads, ROUNDS, starts=False)

        other_rels = {}

        def read_flag(eng):
            eng.wait_ge(S["flag_set"], 1)
            other_rels[eng] = eng.value_load(flag[0:1, 0:1], min_val=0, max_val=1)

        prepared = {}
        block = ctx.enter_context(nc.Block())

        @block.sync
        def _(sp):
            for dst, src in ((cst, const_d), (wts, w_d), (cols, col_d), (spl, split_d), (rows, row_d)):
                sp.dma_start(dst[:], src).then_inc(params_loaded, 16)
            for c in range(CHAINS):
                sp.dma_start(x0[c][:], x_d[:, c * PER_GROUP:(c + 1) * PER_GROUP, :]).then_inc(x_loaded[c], 16)
                sp.dma_start(adj[c][:], adj_d[:, c * PER_GROUP:(c + 1) * PER_GROUP, :]).then_inc(adj_loaded[c], 16)
            sp.dma_start(rel_w[:], rel_w_d).then_inc(rel_w_loaded, 16)
            for k in range(SCANS):
                if k >= 2:
                    sp.wait_ge(S["scan_step"], k - 1)
                sp.dma_start(scan[k % 2][:], adj_d[:, k * SCAN:(k + 1) * SCAN, :]).then_inc(scan_loaded[k % 2], 16)
            with sp.Fori(0, ROUNDS - 1) as r:
                done = [sp.to_reg(r * CHAINS + (c + 1)) for c in range(CHAINS)]
                for c in range(CHAINS):
                    sp.wait_ge(params_loaded, 16 * 5)
                    sp.wait_ge(S["l0_res"], done[c])
                    sp.wait_ge(S["masks"], done[c])
                    at = bass.ds(r * (CHAINS * PER_GROUP) + (CHAINS + c) * PER_GROUP, PER_GROUP)
                    sp.dma_start(x0[c][:], x_d[:, at, :]).then_inc(x_loaded[c], 16)
                    sp.dma_start(adj[c][:], adj_d[:, at, :]).then_inc(adj_loaded[c], 16)

        @block.vector
        def _(dve):
            steps = [0]

            def prep(ins):
                steps[0] += 1
                ins.then_inc(S["prep_step"], 1)

            def settled():
                dve.wait_ge(S["prep_step"], steps[0])

            v = nc.vector
            prep(v.memset(a0s[:], 0.0))
            prep(v.memset(a3s[:], 0.0))
            prep(v.memset(ones_h[:], 1.0))
            prep(v.memset(slots0[:], 0.0))
            prep(v.memset(slots3[:], 0.0))
            settled()
            dve.wait_ge(params_loaded, 16 * 5)
            for part in range(3):
                prep(v.tensor_copy(a0s[:, part:part + 1], col("a0_src")))
                prep(v.tensor_copy(a0s[:, 3 + part:4 + part], col("a0_dst")))
                prep(v.tensor_scalar(a3s[:, 0, 4 * part:4 * part + 4], head_of, col("a3_src"), None, ALU.mult))
                prep(v.tensor_scalar(a3s[:, 0, 12 + 4 * part:16 + 4 * part], head_of, col("a3_dst"), None, ALU.mult))
            prep(v.tensor_scalar(w1a[:], wt("W1T"), col("ln1_w"), None, ALU.mult))
            prep(v.tensor_scalar(w2a[:], wt("W2T"), col("ln2_w"), None, ALU.mult))
            prep(v.tensor_scalar(wl_half[:], wt("WlT"), 0.5, None, ALU.mult))
            prep(v.tensor_copy(ln_b_wide[:, 0, :], col("ln1_b").broadcast_to([P, P])))
            prep(v.tensor_copy(ln_b_wide[:, 1, :], col("ln2_b").broadcast_to([P, P])))
            settled()
            prep(v.tensor_copy(a3s[:, 1:PER_GROUP, :], a3s[:, 0:1, :].broadcast_to([P, PER_GROUP - 1, 32])))
            prepared["operands"] = steps[0]
            prep(v.tensor_scalar(big_gat[:], ident, NEG_GAT, None, ALU.mult))
            prep(v.tensor_scalar(big_att[:], ident, NEG_ATT, None, ALU.mult))
            prep(v.tensor_copy(sel0[:], cst[:, P + HEADS:P + HEADS + W].rearrange("p (a k) -> p a k", a=4)))
            prep(v.tensor_copy(sel3[:], cst[:, P + HEADS + W:P + HEADS + 2 * W].rearrange("p (a k) -> p a k", a=4)))
            prep(v.tensor_scalar(bias_f[:, 2, :], row("b_loop"), 0.5, None, ALU.mult))
            prep(v.tensor_copy(bias_f[:, 3:5, :], rows[:, 3:5, :]))
            dve.wait_ge(S["prep_pe"], 1)
            prep(v.tensor_scalar(qk[:], bank_a[0][:, 0:P], float(P) ** -0.5, None, ALU.mult))
            prep(v.tensor_copy(gate[:], bank_a[0][:, P:2 * P]))
            for k, b in enumerate(("b1", "b2")):
                prep(v.tensor_tensor(bias_f[:, k, :], bank_a[0][:, (2 + k) * P:(3 + k) * P], row(b), ALU.add))
            for g in range(PER_GROUP):
                prep(v.tensor_scalar(slots0[:, g, 32 * g:32 * g + 32], bank_b[0][:, 0:32], ALPHA, None, ALU.mult))
                prep(v.tensor_scalar(slots3[:, g, 32 * g:32 * g + 32], bank_b[0][:, 32:64], ALPHA, None, ALU.mult))
            prep(v.tensor_scalar(kz3[:], bank_b[0][:, 64:65], ALPHA, None, ALU.mult))
            prepared["matrices"] = steps[0]
            settled()

            def step(u, name, after, op):
                for before in after:
                    dve.wait_ge(u.sem(before), u.count(before))
                op().then_inc(u.sem(name), 1)

            def split(u, layer, k, src, dst, selector):
                c = u.c
                if (yield layer + "_eh"):
                    step(u, layer + "_eh", [layer + "_ef"], lambda: v.tensor_copy(e_h[c][:], e_f[c][:]))
                if (yield layer + "_er"):
                    step(u, layer + "_er", [layer + "_eh"], lambda: v.scalar_tensor_tensor(
                        e_r[c][:], e_h[c][:], spl[:, k:k + 1], e_f[c][:], ALU.mult, ALU.add))
                if (yield layer + "_eh2"):
                    step(u, layer + "_eh2", [layer + "_er"], lambda: v.tensor_copy(e_h2[c][:], e_r[c][:]))
                if (yield layer + "_parts"):
                    step(u, layer + "_parts", [layer + "_eh2"], lambda: v.scalar_tensor_tensor(
                        e_parts[c][:], e_h2[c][:], spl[:, k + 1:k + 2], e_r[c][:], ALU.mult, ALU.add))
                if (yield layer + "_row"):
                    step(u, layer + "_row", [layer + "_parts"], lambda: v.tensor_scalar(
                        e_row[c][:], e_parts[c][:], vec(dst), vec(src), ALU.mult, ALU.add))
                if (yield layer + "_rhs"):
                    step(u, layer + "_rhs", [layer + "_row"], lambda: v.tensor_tensor(
                        e_rhs[c][:], e_row[c][:].unsqueeze(1).broadcast_to([P, 4, P]), selector[:], ALU.mult))
                if (yield layer + "_lhs"):
                    step(u, layer + "_lhs", [layer + "_parts"], lambda: v.tensor_scalar(
                        e_lhs[c][:], e_parts[c][:], vec(src), vec(dst), ALU.mult, ALU.add))

            def layer_norm(u, norm, after, src, dst, eps=EPS):
                c = u.c
                if (yield norm + "_stats"):
                    dve.wait_ge(u.sem(after), u.count(after))
                    for k in range(2):
                        last = v.bn_stats(stats[c][:, k, :, :].rearrange("p a s -> p (a s)"),
                                          src[:, 2 * k:2 * k + 2, :].rearrange("p g k -> p k g"))
                    last.then_inc(u.sem(norm + "_stats"), 1)
                if (yield norm + "_veps"):
                    step(u, norm + "_veps", [norm + "_stats"], lambda: v.tensor_scalar(
                        veps[c][:], stats[c][:, :, :, 2:3].rearrange("p a b o -> p (a b o)"), 1.0 / P, eps, ALU.mult, ALU.add))
                if norm in ACT_NORMS and (yield norm + "_off"):
                    step(u, norm + "_off", [norm + "_rstd"], lambda: v.scalar_tensor_tensor(
                        offset[c][:], stats[c][:, 1, :, 1:2].rearrange("p b o -> p (b o)"), -1.0, rstd[c][:, 2:4], ALU.mult, ALU.mult))
                if (yield norm + "_x"):
                    dve.wait_ge(u.sem(norm + "_rstd"), u.count(norm + "_rstd"))
                    for g in range(PER_GROUP // 2 if norm in SHARED_NORMS else PER_GROUP):
                        last = v.tensor_scalar(dst[:, g, :], src[:, g, :], mean_of(c, g), rstd_at(c, g),
                                               ALU.subtract, ALU.mult)
                    last.then_inc(u.sem(norm + "_x"), 1)

            def look():
                yield BIASES_DUE
                prep(v.tensor_copy(bias_h[:], bias_f[:]))
                settled()
                prep(v.scalar_tensor_tensor(bias_r[:], bias_h[:], vec("b_s1"), bias_f[:], ALU.mult, ALU.add))
                settled()
                prep(v.tensor_copy(bias_h[:], bias_r[:]))
                settled()
                prep(v.scalar_tensor_tensor(bias_l[:], bias_h[:], vec("b_s2"), bias_r[:], ALU.mult, ALU.add))
                settled()
                prep(v.tensor_scalar(bias_parts[:], bias_l[:], vec("b_keep"), None, ALU.mult))
                prepared["biases"] = steps[0]
                for k in range(SCANS):
                    yield 2 * k + 5
                    dve.wait_ge(scan_loaded[k % 2], 16 * (k // 2 + 1))
                    v.tensor_reduce(scan_max[:, k:k + 1], scan[k % 2][:].rearrange("p a k -> p (a k)"), AX_X,
                                    ALU.max).then_inc(S["scan_step"], 1)
                yield 36
                dve.wait_ge(S["scan_step"], SCANS)
                v.tensor_reduce(any_max[:], scan_max[:], AX_X, ALU.max).then_inc(S["scan_step"], 1)
                yield 40
                dve.wait_ge(S["scan_row"], 1)
                v.tensor_reduce(top[:], bank_a[2][0:1, 0:P], AX_X, ALU.max).then_inc(S["scan_step"], 1)
                dve.wait_ge(S["scan_step"], SCANS + 2)
                v.tensor_scalar(flag[:], top[:], float(FIRST_REL - 1), None, ALU.is_gt).then_inc(S["flag_set"], 1)
                yield FLAG_READ
                read_flag(dve)

            def relations(u):
                c = u.c
                adj_r = scan[0][:]
                dve.wait_ge(rel_adj_loaded, u.times(16, 16))
                v.tensor_copy(xb[c][:], adj_r)
                v.memset(x3[c][:], 0.0).then_inc(S["rel_zero"], 1)
                dve.wait_ge(S["rel_zero"], u.done())
                v.memset(rel_id[:], float(FIRST_REL)).then_inc(S["rel_id_set"], 1)
                with dve.Fori(0, RELS) as r:
                    id_set = u.nth(RELS + 1, 0, r)
                    used, done = ([u.nth(times, d, r * 2) for d in range(2)] for times in (2 * RELS + 1, 2 * RELS))
                    loaded = u.loads(RELS, r)
                    dve.wait_ge(S["rel_id_set"], id_set)
                    dve.wait_ge(rel_b_loaded, loaded)
                    dve.wait_ge(S["rel_g"], u.nth(2, 1))
                    dve.wait_ge(S["rel_adjT"], u.done())
                    for d, (h, g, a) in enumerate(((val, qT, x1), (sc, pr, None))):
                        def wide(k):
                            return rel_b[:, 2 * d + k, :].unsqueeze(1).broadcast_to([P, PER_GROUP, P])
                        if d == 1:
                            dve.wait_ge(S["rel_v"], done[0])
                        v.tensor_tensor(t1[c][:], g[c][:], wide(1), ALU.add).then_inc(S["rel_u"], 1)
                        dve.wait_ge(S["rel_mm"], used[d])
                        v.tensor_tensor(pT[c][:], h[c][:], wide(0), ALU.add).then_inc(S["rel_a"], 1)
                        v.tensor_scalar(xb[c][:], a[c][:] if a else adj_r, rel_id[:, 0:1], 0.5, ALU.is_equal, ALU.mult)
                        dve.wait_ge(S["rel_a"], done[d])
                        dve.wait_ge(S["rel_th"], done[d])
                        v.scalar_tensor_tensor(pT[c][:], t1[c][:], 1.0, pT[c][:], ALU.add, ALU.mult).then_inc(S["rel_v"], 1)
                    dve.wait_ge(S["rel_v"], done[1])
                    v.tensor_scalar(rel_id[:], rel_id[:], 1.0, None, ALU.add).then_inc(S["rel_id_set"], 1)

            def group(u):
                c = u.c
                if (yield "pos_mask"):
                    dve.wait_ge(adj_loaded[c], u.chain_load())
                    v.tensor_scalar(pos_m1[c][:], adj[c][:], 0.0, -1.0, ALU.is_gt, ALU.add).then_inc(S["pos_mask"], 1)
                if (yield "masks"):
                    v.tensor_scalar(zero_m[c][:], adj[c][:], 0.0, -1.0, ALU.is_equal, ALU.mult)
                    v.tensor_scalar(one_m[c][:], adj[c][:], 1.0, None, ALU.is_equal).then_inc(S["masks"], 1)
                yield from split(u, "l0", 0, "src0", "dst0", sel0)
                if (yield "l0_leaky"):
                    step(u, "l0_leaky", ["l0_relu"], lambda: v.tensor_tensor(sc[c][:], bank(bank_a, c), sc[c][:], ALU.add))
                if (yield "l0_max"):
                    step(u, "l0_max", ["l0_leaky"], lambda: v.tensor_reduce(nmax[c][:], sc[c][:], AX_X, ALU.max, negate=True))
                if (yield "l0_rs"):
                    step(u, "l0_rs", ["l0_exp"], lambda: v.reciprocal(rsum[c][:], rowsum[c][:]))
                if (yield "l0_gated"):
                    step(u, "l0_gated", ["l0_act"], lambda: v.scalar_tensor_tensor(
                        t2[c][:], t2[c][:], 1.0, t1[c][:], ALU.min, ALU.max))
                yield from layer_norm(u, "na", "l0_res", t2[c], x1[c])
                if (yield "l1_max"):
                    step(u, "l1_max", ["l1_sp"], lambda: v.tensor_reduce(nmax[c][:], bank(bank_a, c), AX_X, ALU.max, negate=True))
                if (yield "l1_rs"):
                    step(u, "l1_rs", ["l1_exp"], lambda: v.reciprocal(rsum[c][:], rowsum[c][:]))
                if (yield "l1_gated"):
                    step(u, "l1_gated", ["l1_act"], lambda: v.scalar_tensor_tensor(
                        t1[c][:], t2[c][:], 1.0, t1[c][:], ALU.add, ALU.mult))
                yield from layer_norm(u, "nb", "l1_gated", t1[c], t2[c], 4 * EPS)
                if (yield "n1_gated"):
                    step(u, "n1_gated", ["n1_th"], lambda: v.scalar_tensor_tensor(
                        t2[c][:], t1[c][:], 1.0, bank(bank_b, c), ALU.add, ALU.mult))
                yield from layer_norm(u, "nc", "n1_gated", t2[c], t1[c], 4 * EPS)
                yield from layer_norm(u, "nd", "n2_hp", bank(bank_b, c), t1[c])
                yield from layer_norm(u, "ne", "l1_res", t2[c], x2[c])
                if (yield "l2_v"):
                    step(u, "l2_v", ["l2_th", "l2_hp"], lambda: v.scalar_tensor_tensor(
                        t2[c][:], t1[c][:], 1.0, bank(bank_b, c), ALU.add, ALU.mult))
                if (yield "relations"):
                    with dve.If(other_rels[dve] > 0):
                        relations(u)

                def residual():
                    step(u, "l2_res", ["l2_out"], lambda: v.scalar_tensor_tensor(
                        t1[c][:], bank(bank_b, c), 0.0, x2[c][:], ALU.max, ALU.add))

                if (yield "l2_res"):
                    with dve.If(other_rels[dve] > 0):
                        step(u, "rel_added", ["l2_out", "rel_extra"], lambda: v.tensor_tensor(
                            bank(bank_b, c), bank(bank_b, c), x3[c][:], ALU.add))
                        dve.wait_ge(S["rel_added"], u.done())
                        residual()
                    with dve.Else():
                        residual()
                yield from layer_norm(u, "nf", "l2_res", t1[c], x3[c])
                yield from split(u, "l3", 2, "src3", "dst3", sel3)
                yield from layer_norm(u, "ng", "l3_res", t1[c], xo[c])

            def heads(u, g):
                c, d = u.c, g % 2
                z = head_bank(u, g)
                outs = z[:, 0:HEADS * HS].rearrange("p (h k) -> p h k", h=HEADS)
                if (yield "h_leaky", g):
                    dve.wait_ge(S["h_relu"], u.graph_done(g))
                    v.tensor_tensor(h_sc[c][d][:], z.rearrange("p (h k) -> p h k", h=HEADS), h_sc[c][d][:], ALU.add).then_inc(S["h_leaky"], 1)
                if (yield "h_max", g):
                    dve.wait_ge(S["h_leaky"], u.graph_done(g))
                    v.tensor_reduce(h_nmax[c][:, d, :], h_sc[c][d][:], AX_X, ALU.max, negate=True).then_inc(S["h_max"], 1)
                if (yield "h_rs", g):
                    dve.wait_ge(S["h_pv"], u.graph_done(g))
                    v.reciprocal(h_rsum[c][:, d, :].unsqueeze(2), outs[:, :, HEAD_C:HS]).then_inc(S["h_rs"], 1)
                if (yield "h_out", g):
                    dve.wait_ge(S["h_rs"], u.graph_done(g))
                    v.tensor_tensor(t1[c][:, g, :].rearrange("p (h k) -> p h k", h=HEADS), outs[:, :, 0:HEAD_C],
                                    h_rsum[c][:, d, :].unsqueeze(2).broadcast_to([P, HEADS, HEAD_C]), ALU.mult).then_inc(S["h_out"], 1)

            run(dve, group, heads, look())

        @block.gpsimd
        def _(pool):
            for c in range(CHAINS):
                nc.gpsimd.memset(h3[c][:, :, :, HEAD_C:HS], 1.0)
            nc.gpsimd.memset(minus_one[:], -1.0)
            nc.gpsimd.memset(half_pow[:], -0.5).then_inc(S["prep_pow"], 1)
            pool.wait_ge(S["prep_pow"], 1)
            pool.wait_ge(S["prep_step"], prepared["matrices"])
            row_wide = [P, PER_GROUP, P]

            def add_to(u, name, after, dst, a, b, op=ALU.add):
                for before in after:
                    pool.wait_ge(u.sem(before), u.count(before))
                nc.gpsimd.tensor_tensor(dst[:], a, b, op).then_inc(u.sem(name), 1)

            def norm_of(u, norm, src, dst):
                c = u.c
                if (yield norm + "_rstd"):
                    add_to(u, norm + "_rstd", [norm + "_veps"], rstd[c], veps[c][:], half_pow[:], ALU.pow)
                if norm in POOL_NORMS:
                    half = slice(PER_GROUP // 2, PER_GROUP)
                    if (yield norm + "_centred"):
                        nc.gpsimd.tensor_tensor(dst[:, half, :], src[:, half, :], stats[c][:, 1, :, 1:2].broadcast_to([P, PER_GROUP // 2, P]),
                                                ALU.subtract).then_inc(u.sem(norm + "_centred"), 1)
                    if (yield norm + "_y"):
                        for before in (norm + "_rstd", norm + "_centred"):
                            pool.wait_ge(u.sem(before), u.count(before))
                        nc.gpsimd.tensor_tensor(dst[:, half, :], dst[:, half, :], rstd[c][:, half].unsqueeze(2).broadcast_to([P, PER_GROUP // 2, P]),
                                                ALU.mult).then_inc(u.sem(norm + "_y"), 1)

            def group(u):
                c = u.c
                if (yield "one_mask"):
                    add_to(u, "one_mask", ["masks"], one_m1[c], one_m[c][:], minus_one[:, 0:1].unsqueeze(2).broadcast_to(row_wide))
                if (yield "l0_res"):
                    add_to(u, "l0_res", ["l0_gated"], t2[c], t2[c][:], x0[c][:])
                yield from norm_of(u, "na", t2[c], x1[c])
                if (yield "xb_ready"):
                    add_to(u, "xb_ready", u.normed("na"), xb[c], x1[c][:], row("lnf_b").unsqueeze(1).broadcast_to(row_wide))
                yield from norm_of(u, "nb", t1[c], t2[c])
                yield from norm_of(u, "nc", t2[c], t1[c])
                yield from norm_of(u, "nd", None, None)
                if (yield "n3_w"):
                    add_to(u, "n3_w", ["nd_x"], t1[c], t1[c][:], row("lnf_w").unsqueeze(1).broadcast_to(row_wide), ALU.mult)
                if (yield "l1_res"):
                    add_to(u, "l1_res", ["n3_w"], t2[c], t1[c][:], xb[c][:])
                yield from norm_of(u, "ne", t2[c], x2[c])
                yield from norm_of(u, "nf", t1[c], x3[c])
                if (yield "l3_res"):
                    pool.wait_ge(S["h_out"], u.graph_done(PER_GROUP - 1))
                    nc.gpsimd.tensor_tensor(t1[c][:], t1[c][:], x3[c][:], ALU.add).then_inc(S["l3_res"], 1)
                yield from norm_of(u, "ng", t1[c], xo[c])
                if (yield "stored"):
                    pool.wait_ge(stored[c], u.chain_load())

            run(pool, group, None)

        @block.scalar
        def _(act):
            act.wait_ge(S["prep_pow"], 1)
            nc.scalar.activation(warm[:], half_pow[:], ACT.Exp).then_inc(S["prep_act"], 1)
            act.wait_ge(S["prep_step"], prepared["matrices"])

            def a_bank(u):
                return bank(bank_a, u.c)

            def b_bank(u):
                return bank(bank_b, u.c)

            def move(u, name, after, dst, src, func=ACT.Copy, **kw):
                act.wait_ge(u.sem(after), u.count(after))
                nc.scalar.activation(dst[:], src, func, **kw).then_inc(S[name], 1)

            def soften(u, layer, src):
                c = u.c
                act.wait_ge(S[layer + "_max"], u.done())
                for g in range(PER_GROUP):
                    last = nc.scalar.activation(pr[c][:, g, :], src[:, g, :], ACT.Exp, bias=nmax[c][:, g:g + 1],
                                                accum_out=rowsum[c][:, g:g + 1])
                last.then_inc(S[layer + "_exp"], 1)

            def weigh(u, layer):
                c = u.c
                act.wait_ge(S[layer + "_rs"], u.done())
                act.wait_ge(S[layer + "_pv"], u.done())
                for g in range(PER_GROUP):
                    last = nc.scalar.activation(t1[c][:, g, :], bank_b[c][:, g * P:(g + 1) * P], ACT.Copy,
                                                scale=rsum[c][:, g:g + 1])
                last.then_inc(S[layer + "_h"], 1)

            def normal(u, norm, src, dst):
                act.wait_ge(u.sem(norm + "_off"), u.count(norm + "_off"))
                for g in range(PER_GROUP // 2, PER_GROUP):
                    last = nc.scalar.activation(dst[:, g, :], src[:, g, :], ACT.Identity, scale=rstd_at(u.c, g),
                                                bias=offset[u.c][:, g - PER_GROUP // 2:g - PER_GROUP // 2 + 1])
                last.then_inc(u.sem(norm + "_y"), 1)

            def look():
                yield FLAG_READ
                read_flag(act)

            def relations(u):
                c = u.c
                act.wait_ge(S["l2_v"], u.done())
                act.dma_start(scan[0][:], adj_d[:, u.graphs(), :]).then_inc(rel_adj_loaded, 16)
                act.wait_ge(S["rel_adjTp"], u.done())
                nc.scalar.activation(x1[c][:], a_bank(u), ACT.Copy).then_inc(S["rel_adjT"], 1)
                for d, (h, g) in enumerate(((val, qT), (sc, pr))):
                    act.wait_ge(S["rel_hTp"], u.nth(2, d))
                    nc.scalar.activation(pT[c][:], a_bank(u), ACT.Copy).then_inc(S["rel_hT"], 1)
                    act.wait_ge(S["rel_gp"], u.nth(2, d))
                    nc.scalar.activation(h[c][:], b_bank(u), ACT.Copy)
                    nc.scalar.activation(g[c][:], a_bank(u), ACT.Copy).then_inc(S["rel_g"], 1)
                with act.Fori(0, RELS) as r:
                    done = [u.nth(2 * RELS, d, r * 2) for d in range(2)]
                    act.wait_ge(S["rel_id_set"], u.nth(RELS + 1, 0, r))
                    act.dma_start(rel_b[:].rearrange("p a k -> p (a k)"), rel_b_d[bass.ds(r, 1), :].broadcast_to([P, 4 * P])).then_inc(rel_b_loaded, 16)
                    for d in range(2):
                        act.wait_ge(S["rel_u"], done[d])
                        nc.scalar.activation(t1[c][:], t1[c][:], ACT.Tanh, scale=0.5).then_inc(S["rel_th"], 1)
                act.wait_ge(S["rel_out"], u.done())
                nc.scalar.activation(x3[c][:], a_bank(u), ACT.Copy).then_inc(S["rel_extra"], 1)

            def group(u):
                c = u.c
                if (yield "l0_xT"):
                    move(u, "l0_xT", "l0_xTp", xT[c], a_bank(u))
                if (yield "l0_ef"):
                    move(u, "l0_ef", "l0_ep", e_f[c], bank_a[c][:, 0:P])
                if (yield "l0_val"):
                    move(u, "l0_val", "l0_valp", val[c], b_bank(u), ACT.Identity, bias=1.0)
                if (yield "l0_relu"):
                    move(u, "l0_relu", "l0_z", sc[c], a_bank(u), ACT.Relu, scale=1 / ALPHA - 1)
                if (yield "l0_exp"):
                    soften(u, "l0", sc[c])
                if (yield "l0_pT"):
                    move(u, "l0_pT", "l0_pTp", pT[c], a_bank(u))
                if (yield "l0_h"):
                    weigh(u, "l0")
                if (yield "l0_act"):
                    move(u, "l0_act", "l0_h", t2[c], t1[c][:], ACT.Exp, bias=-1.0)
                if "na" in ACT_NORMS and (yield "na_y"):
                    normal(u, "na", t2[c], x1[c])
                if (yield "l1_xT"):
                    move(u, "l1_xT", "l1_xTp", xT[c], a_bank(u))
                if (yield "l1_qT"):
                    move(u, "l1_qT", "l1_qTp", qT[c], b_bank(u))
                if (yield "l1_val"):
                    move(u, "l1_val", "l1_valp", val[c], b_bank(u))
                if (yield "l1_exp"):
                    soften(u, "l1", a_bank(u))
                if (yield "l1_pT"):
                    move(u, "l1_pT", "l1_pTp", pT[c], a_bank(u))
                if (yield "l1_h"):
                    weigh(u, "l1")
                if (yield "l1_act"):
                    move(u, "l1_act", "l1_h", t2[c], t1[c][:], ACT.Tanh, scale=0.5)
                if "nb" in ACT_NORMS and (yield "nb_y"):
                    normal(u, "nb", t1[c], t2[c])
                if (yield "n1_xT"):
                    move(u, "n1_xT", "n1_xTp", xT[c], a_bank(u))
                if (yield "n1_th"):
                    move(u, "n1_th", "n1_hp", t1[c], b_bank(u), ACT.Tanh, scale=0.5)
                if "nc" in ACT_NORMS and (yield "nc_y"):
                    normal(u, "nc", t2[c], t1[c])
                if (yield "n2_xT"):
                    move(u, "n2_xT", "n2_xTp", xT[c], a_bank(u))
                if "ne" in ACT_NORMS and (yield "ne_y"):
                    normal(u, "ne", t2[c], x2[c])
                if (yield "l2_xT"):
                    move(u, "l2_xT", "l2_xTp", xT[c], a_bank(u))
                if (yield "l2_th"):
                    move(u, "l2_th", "l2_gp", t1[c], a_bank(u), ACT.Tanh, scale=0.5)
                if (yield "relations"):
                    with act.If(other_rels[act] > 0):
                        relations(u)
                if "nf" in ACT_NORMS and (yield "nf_y"):
                    normal(u, "nf", t1[c], x3[c])
                if (yield "l3_xT"):
                    move(u, "l3_xT", "l3_xTp", xT[c], a_bank(u))
                if (yield "l3_ef"):
                    move(u, "l3_ef", "l3_ep", e_f[c], bank_a[c][:, 0:P], ACT.Identity, bias=kz3[:, 0:1])
                if (yield "l3_h"):
                    act.wait_ge(S["l3_hp"], u.done())
                    nc.scalar.activation(h3[c][:, :, :, 0:HEAD_C], bank_b[c][:, :].rearrange("p (g h k) -> p g h k", g=PER_GROUP, h=HEADS),
                                         ACT.Copy).then_inc(S["l3_h"], 1)
                if "ng" in ACT_NORMS and (yield "ng_y"):
                    normal(u, "ng", t1[c], xo[c])
                if (yield "store"):
                    for before in u.normed("ng"):
                        act.wait_ge(u.sem(before), u.count(before))
                    act.dma_start(out_d[:, u.graphs(), :], xo[c][:]).then_inc(stored[c], 16)

            def heads(u, g):
                c, d = u.c, g % 2
                z = head_bank(u, g).rearrange("p (h k) -> p h k", h=HEADS)
                if (yield "h_relu", g):
                    act.wait_ge(S["h_z"], u.graph_done(g))
                    nc.scalar.activation(h_sc[c][d][:], z, ACT.Relu, scale=1 / ALPHA - 1).then_inc(S["h_relu"], 1)
                if (yield "h_exp", g):
                    act.wait_ge(S["h_max"], u.graph_done(g))
                    for h in range(HEADS):
                        last = nc.scalar.activation(h_pr[c][d][:, h, :], h_sc[c][d][:, h, :], ACT.Exp, bias=h_nmax[c][:, d, h:h + 1])
                    last.then_inc(S["h_exp"], 1)
                if (yield "h_pT", g):
                    act.wait_ge(S["h_pTp"], u.graph_done(g))
                    nc.scalar.activation(h_pT[c][d][:], z, ACT.Copy).then_inc(S["h_pT"], 1)

            run(act, group, heads, look())

        @block.tensor
        def _(pe):
            t = nc.tensor
            pe.wait_ge(params_loaded, 16 * 5)
            pe.wait_ge(S["prep_step"], prepared["operands"])
            t.matmul(bank_a[0][:, 0:P], wt("Wq"), wt("Wk"), start=True, stop=True)
            t.matmul(bank_a[0][:, P:2 * P], wt("Wl"), wt("WgT"), start=True, stop=True)
            t.matmul(bank_a[0][:, 2 * P:3 * P], ln_b_wide[:, 0, :], wt("W1T"), start=True, stop=True)
            t.matmul(bank_a[0][:, 3 * P:4 * P], ln_b_wide[:, 1, :], wt("W2T"), start=True, stop=True)
            t.matmul(bank_b[0][:, 0:32], wt("W0T"), a0s[:], start=True, stop=True)
            t.matmul(bank_b[0][:, 32:64], wt("W3"), a3s[:, 0, :], start=True, stop=True)
            t.matmul(bank_b[0][:, 64:65], a3s[:].rearrange("p g s -> p (g s)"), col("b3"),
                     start=True, stop=True).then_inc(S["prep_pe"], 1)
            pe.wait_ge(S["prep_step"], prepared["matrices"])
            pe.wait_ge(S["prep_pow"], 1)

            def cut(banks, c, g):
                return banks[c][:, g * P:(g + 1) * P]

            def transposes(u, name, after, src):
                for before in after:
                    pe.wait_ge(u.sem(before), u.count(before))
                for g in range(PER_GROUP):
                    last = t.transpose(cut(bank_a, u.c, g), src[u.c][:, g, :], ident)
                last.then_inc(S[name], 1)

            def project(u, name, after, banks, weights, bias=None):
                c = u.c
                for before in after:
                    pe.wait_ge(u.sem(before), u.count(before))
                if bias is not None:
                    t.matmul(bank(banks, c), ones_h[:], bias_parts[:, bias, :].unsqueeze(1).broadcast_to([P, PER_GROUP, P]),
                             start=True, stop=False, skip_group_check=True)
                for g in range(PER_GROUP):
                    last = t.matmul(cut(banks, c, g), xT[c][:, g, :], weights, start=bias is None and g == 0,
                                    stop=g == PER_GROUP - 1, skip_group_check=True)
                last.then_inc(S[name], 1)

            def logits(u, name, after, slots):
                for before in after:
                    pe.wait_ge(u.sem(before), u.count(before))
                for g in range(PER_GROUP):
                    last = t.matmul(bank_a[u.c][:, 0:P], slots[:, g, :], xT[u.c][:, g, :], start=g == 0, stop=g == PER_GROUP - 1)
                last.then_inc(S[name], 1)

            def attend(u, layer):
                c = u.c
                pe.wait_ge(S[layer + "_pT"], u.done())
                pe.wait_ge(S[layer + "_val"], u.done())
                for g in range(PER_GROUP):
                    last = t.matmul(cut(bank_b, c, g), pT[c][:, g, :], val[c][:, g, :], start=True, stop=True)
                last.then_inc(S[layer + "_pv"], 1)

            def look():
                yield BIASES_DUE + 8
                pe.wait_ge(S["prep_step"], prepared["biases"])
                yield 38
                pe.wait_ge(S["scan_step"], SCANS + 1)
                t.transpose(bank_a[2][0:1, 0:P], any_max[:], ident).then_inc(S["scan_row"], 1)
                yield FLAG_READ
                read_flag(pe)

            def relations(u):
                c = u.c
                pe.wait_ge(rel_w_loaded, 16)
                pe.wait_ge(S["l2_v"], u.done())
                pe.wait_ge(S["rel_zero"], u.done())
                for g in range(PER_GROUP):
                    last = t.transpose(cut(bank_a, c, g), xb[c][:, g, :], ident)
                last.then_inc(S["rel_adjTp"], 1)
                for d in range(2):
                    if d == 0:
                        pe.wait_ge(S["rel_adjT"], u.done())
                    else:
                        pe.wait_ge(S["rel_g"], u.nth(2, 0))
                    t.matmul(bank_a[c][:, :], rel_w[:, 2 * d, :], flat(xT[c]), start=True, stop=True).then_inc(S["rel_hTp"], 1)
                    for g in range(PER_GROUP):
                        t.matmul(cut(bank_b, c, g), xT[c][:, g, :], rel_w[:, 2 * d, :], start=True, stop=True)
                    pe.wait_ge(S["rel_hT"], u.nth(2, d))
                    for g in range(PER_GROUP):
                        last = t.matmul(cut(bank_a, c, g), pT[c][:, g, :], rel_w[:, 2 * d + 1, :], start=True, stop=True)
                    last.then_inc(S["rel_gp"], 1)
                pe.wait_ge(S["rel_g"], u.nth(2, 1))
                pe.wait_ge(S["rel_zero"], u.done())
                t.matmul(bank_a[c][:, :], ident, flat(x3[c]), start=True, stop=False, skip_group_check=True).then_inc(S["rel_mm"], 1)
                with pe.Fori(0, RELS) as r:
                    done = [u.nth(2 * RELS, d, r * 2) for d in range(2)]
                    for d in range(2):
                        pe.wait_ge(S["rel_v"], done[d])
                        for g in range(PER_GROUP):
                            last = t.matmul(cut(bank_a, c, g), xb[c][:, g, :], pT[c][:, g, :], start=False, stop=False, skip_group_check=True)
                        last.then_inc(S["rel_mm"], 1)
                t.matmul(bank_a[c][:, :], ident, flat(x3[c]), start=False, stop=True, skip_group_check=True).then_inc(S["rel_out"], 1)

            def group(u):
                c = u.c
                if (yield "l0_xTp"):
                    pe.wait_ge(x_loaded[c], u.chain_load())
                    for g in range(PER_GROUP):
                        last = t.transpose(cut(bank_a, c, g), x0[c][:, g, :], ident)
                    last.then_inc(S["l0_xTp"], 1)
                if (yield "l0_ep"):
                    logits(u, "l0_ep", ["l0_xT"], slots0)
                if (yield "l0_valp"):
                    project(u, "l0_valp", [], bank_b, wt("W0"))
                if (yield "l0_z"):
                    for before in ("l0_rhs", "l0_lhs", "pos_mask"):
                        pe.wait_ge(u.sem(before), u.count(before))
                    t.matmul(bank_a[c][:, :], e_lhs[c][:], flat(e_rhs[c]), start=True, stop=False)
                    t.matmul(bank_a[c][:, :], big_gat[:], flat(pos_m1[c]), start=False, stop=True).then_inc(S["l0_z"], 1)
                if (yield "l0_pTp"):
                    transposes(u, "l0_pTp", ["l0_exp"], pr)
                if (yield "l0_pv"):
                    attend(u, "l0")
                if (yield "l1_xTp"):
                    transposes(u, "l1_xTp", u.normed("na"), x1)
                if (yield "l1_qTp"):
                    pe.wait_ge(S["l1_xT"], u.done())
                    pe.wait_ge(S["l0_h"], u.done())
                    t.matmul(bank_b[c][:, :], qk[:], flat(xT[c]), start=True, stop=True).then_inc(S["l1_qTp"], 1)
                if (yield "l1_sp"):
                    pe.wait_ge(S["l1_qT"], u.done())
                    pe.wait_ge(S["masks"], u.done())
                    for g in range(PER_GROUP):
                        t.matmul(cut(bank_a, c, g), qT[c][:, g, :], xT[c][:, g, :], start=g == 0, stop=False, skip_group_check=True)
                    t.matmul(bank_a[c][:, :], big_att[:], flat(zero_m[c]),
                             start=False, stop=True, skip_group_check=True).then_inc(S["l1_sp"], 1)
                if (yield "l1_valp"):
                    project(u, "l1_valp", [], bank_b, wt("WvT"))
                if (yield "l1_pTp"):
                    transposes(u, "l1_pTp", ["l1_exp"], pr)
                if (yield "l1_pv"):
                    attend(u, "l1")
                if (yield "n1_xTp"):
                    transposes(u, "n1_xTp", u.normed("nb"), t2)
                if (yield "n1_hp"):
                    project(u, "n1_hp", ["n1_xT", "l1_h"], bank_b, w1a[:], bias=0)
                if (yield "n2_xTp"):
                    transposes(u, "n2_xTp", u.normed("nc"), t1)
                if (yield "n2_hp"):
                    project(u, "n2_hp", ["n2_xT", "n1_gated"], bank_b, w2a[:], bias=1)
                if (yield "l2_xTp"):
                    transposes(u, "l2_xTp", u.normed("ne"), x2)
                if (yield "l2_gp"):
                    project(u, "l2_gp", ["l2_xT"], bank_a, gate[:], bias=3)
                if (yield "l2_hp"):
                    project(u, "l2_hp", ["nd_x"], bank_b, wl_half[:], bias=2)
                if (yield "relations"):
                    with pe.If(other_rels[pe] > 0):
                        relations(u)
                if (yield "l2_out"):
                    pe.wait_ge(S["l2_v"], u.done())
                    for g in range(PER_GROUP):
                        last = t.matmul(cut(bank_b, c, g), one_m[c][:, g, :], t2[c][:, g, :], start=True, stop=True)
                    last.then_inc(S["l2_out"], 1)
                if (yield "l3_xTp"):
                    transposes(u, "l3_xTp", u.normed("nf"), x3)
                if (yield "l3_ep"):
                    logits(u, "l3_ep", ["l3_xT"], slots3)
                if (yield "l3_hp"):
                    project(u, "l3_hp", ["l2_res"], bank_b, wt("W3T"), bias=4)

            def heads(u, g):
                c, d = u.c, g % 2
                z = head_bank(u, g)
                quad = slice(32 * g, 32 * g + 32)
                if (yield "h_z", g):
                    if g == 0:
                        for before in ("l3_rhs", "l3_lhs", "one_mask"):
                            pe.wait_ge(u.sem(before), u.count(before))
                    elif g == 1:
                        pe.wait_ge(S["l3_h"], u.done())
                    else:
                        pe.wait_ge(S["h_out"], u.graph_done(g - 2))
                    t.matmul(z, e_lhs[c][quad, :], e_rhs[c][quad, :, :].rearrange("p a k -> p (a k)"), start=True, stop=False)
                    t.matmul(z.rearrange("p (h k) -> p h k", h=HEADS), big_gat[:], one_m1[c][:, g, :].unsqueeze(1).broadcast_to([P, HEADS, P]),
                             start=False, stop=True).then_inc(S["h_z"], 1)
                if (yield "h_pTp", g):
                    pe.wait_ge(S["h_exp"], u.graph_done(g))
                    for h in range(HEADS):
                        last = t.transpose(z[:, h * P:(h + 1) * P], h_pr[c][d][:, h, :], ident)
                    last.then_inc(S["h_pTp"], 1)
                if (yield "h_pv", g):
                    pe.wait_ge(S["h_pT"], u.graph_done(g))
                    if g == 0:
                        pe.wait_ge(S["l3_h"], u.done())
                    for h in range(HEADS):
                        last = t.matmul(z[:, h * HS:(h + 1) * HS], h_pT[c][d][:, h, :], h3[c][:, g, h, :], start=True, stop=True)
                    last.then_inc(S["h_pv"], 1)
                if g >= 2 and (yield "released", g - 2):
                    pe.wait_ge(S["h_out"], u.graph_done(g))

            run(pe, group, heads, look())


def kernel(**inputs):
    import concourse.bacc as bacc
    from concourse.bass_utils import run_bass_kernel_spmd

    def f(name):
        return np.asarray(inputs[name])

    arrays = {
        "x_in": np.ascontiguousarray(f("x").transpose(1, 0, 2)),
        "adj_in": np.ascontiguousarray(f("adj").transpose(1, 0, 2)),
        "weights_in": np.ascontiguousarray(np.stack([
            f("L0_gnn_W"), f("L0_gnn_W").T, f("L1_gnn_Wq"), f("L1_gnn_Wk"), f("L1_gnn_Wv").T, f("L1_gnn_W1").T,
            f("L1_gnn_W2").T, f("L2_gnn_W_loop"), f("L2_gnn_W_loop").T, f("L2_gnn_Wg_loop").T,
            f("L3_gnn_W"), f("L3_gnn_W").T], axis=1)),
        "columns_in": np.ascontiguousarray(np.stack([
            f("L0_gnn_a")[:P, 0], f("L0_gnn_a")[P:, 0], f("L1_gnn_ln1_w"), f("L1_gnn_ln1_b"), f("L1_gnn_ln2_w"),
            f("L1_gnn_ln2_b"), f("L3_gnn_a")[:, :HEAD_C].reshape(P), f("L3_gnn_a")[:, HEAD_C:].reshape(P),
            f("L3_gnn_b")], axis=1)),
        "rows_in": np.ascontiguousarray(np.broadcast_to(np.stack([
            f("L1_gnn_b1"), f("L1_gnn_b2"), f("L2_gnn_b_loop")[0], f("L2_gnn_bg_loop")[0], f("L3_gnn_b"),
            f("L1_gnn_lnf_w"), f("L1_gnn_lnf_b")])[None], (P, len(ROWS), P))),
        "consts_in": constants(),
        "split_in": split_vectors(),
        "rel_weights_in": np.ascontiguousarray(np.stack([
            f("L2_gnn_W_fwd").T, f("L2_gnn_Wg_fwd").T, f("L2_gnn_W_bwd").T, f("L2_gnn_Wg_bwd").T], axis=1)),
        "rel_biases_in": np.ascontiguousarray(np.concatenate([
            f("L2_gnn_b_fwd"), f("L2_gnn_bg_fwd"), f("L2_gnn_b_bwd"), f("L2_gnn_bg_bwd")], axis=1)),
    }
    nc = bacc.Bacc("TRN2", target_bir_lowering=False, num_devices=1)
    args = [nc.dram_tensor(name, a.shape, mybir.dt.from_np(a.dtype), kind="ExternalInput").ap() for name, a in arrays.items()]
    out = nc.dram_tensor("out", (P, GRAPHS, P), F32, kind="ExternalOutput").ap()
    graph_layers_kernel(nc, *args, out)
    r = run_bass_kernel_spmd(nc, [arrays], core_ids=[0])
    return np.ascontiguousarray(r.results[0]["out"].transpose(1, 0, 2))
```
